# Optimizing a Trainium2 kernel written in Bass

```python
import numpy as np
import jax
import jax.numpy as jnp

def _softmax(x, axis=-1):
    return jax.nn.softmax(x, axis=axis)

def _gelu(x):
    return jax.nn.gelu(x, approximate=True)

def _silu(x):
    return jax.nn.silu(x)

def _sigmoid(x):
    return jax.nn.sigmoid(x)

def _layernorm(x, axis=-1, eps=1e-05):
    m = jnp.mean(x, axis=axis, keepdims=True)
    v = jnp.var(x, axis=axis, keepdims=True)
    return (x - m) / jnp.sqrt(v + eps)

def _scatter_add(tgt, idx, src, axis=0):
    return tgt.at[idx].add(src)

def _segment_sum(src, seg, n):
    return jax.ops.segment_sum(src, seg, n)
kernel_name = 'mk_adaln_d1_jaxref_r8_7ebc10'

def setup_inputs(seed: int=0):
    np.random.seed(seed)
    _w = jnp.asarray

    def _L0_attn_setup():
        import jax, jax.numpy as jnp
        import numpy as np
        import math
        D_MODEL = 512
        NUM_HEADS = 32
        NUM_KV_HEADS = 8
        HEAD_DIM = D_MODEL // NUM_HEADS
        GROUP = NUM_HEADS // NUM_KV_HEADS
        SEQ_LEN = 256
        BATCH = 2
        ROPE_THETA = 10000.0

        def apply_rope(x, start_pos=0):
            b, h, s, hd = x.shape
            inv_freq = 1.0 / ROPE_THETA ** (jnp.arange(0, hd, 2, dtype=jnp.float32) / hd)
            pos = jnp.arange(start_pos, start_pos + s, dtype=jnp.float32)
            ang = pos[:, None] * inv_freq[None, :]
            cos = jnp.cos(ang).astype(x.dtype)
            sin = jnp.sin(ang).astype(x.dtype)
            xr = x[..., 0::2]
            xi = x[..., 1::2]
            out_r = xr * cos - xi * sin
            out_i = xr * sin + xi * cos
            return jnp.stack([out_r, out_i], axis=-1).reshape(b, h, s, hd)
        key = jax.random.key(seed)
        ks = jax.random.split(key, 5)
        qkv_dim = HEAD_DIM * (NUM_HEADS + 2 * NUM_KV_HEADS)
        scale = 1.0 / math.sqrt(D_MODEL)
        return {'x': jax.random.normal(ks[0], (BATCH, SEQ_LEN, D_MODEL), jnp.float32), 'w_qkv': jax.random.normal(ks[1], (qkv_dim, D_MODEL), jnp.float32) * scale, 'b_qkv': jax.random.normal(ks[2], (qkv_dim,), jnp.float32) * 0.01, 'w_o': jax.random.normal(ks[3], (D_MODEL, D_MODEL), jnp.float32) * scale, 'b_o': jax.random.normal(ks[4], (D_MODEL,), jnp.float32) * 0.01}
    _L0_attn_in = _L0_attn_setup()

    def _L0_ffn_setup():
        import jax, jax.numpy as jnp
        import numpy as np
        NUM_EXPERTS = 32
        D_MODEL = 512
        TOP_K = 2
        key = jax.random.key(seed)
        k1, k2, k3, k4 = jax.random.split(key, 4)
        x = jax.random.normal(k1, (2, 256, D_MODEL), dtype=jnp.float32)
        gate_w = jax.random.normal(k2, (NUM_EXPERTS, D_MODEL), dtype=jnp.float32) * 0.02
        expert_w = jax.random.normal(k3, (NUM_EXPERTS, D_MODEL, D_MODEL), dtype=jnp.float32) * 0.02
        expert_b = jax.random.normal(k4, (NUM_EXPERTS, D_MODEL), dtype=jnp.float32) * 0.02
        return {'x': x, 'gate_w': gate_w, 'expert_w': expert_w, 'expert_b': expert_b}
    _L0_ffn_in = _L0_ffn_setup()
    _L0_c = _w((lambda *s: np.random.randn(*s).astype(np.float32) * 0.05)(4, 512))
    _L0_wmod = _w((lambda *s: np.random.randn(*s).astype(np.float32) * 0.05)(512, 6 * 512) * 512 ** (-0.5))
    _d = {'L0_attn_x': _L0_attn_in['x'], 'L0_attn_w_qkv': _L0_attn_in['w_qkv'], 'L0_attn_b_qkv': _L0_attn_in['b_qkv'], 'L0_attn_w_o': _L0_attn_in['w_o'], 'L0_attn_b_o': _L0_attn_in['b_o'], 'L0_ffn_gate_w': _L0_ffn_in['gate_w'], 'L0_ffn_expert_w': _L0_ffn_in['expert_w'], 'L0_ffn_expert_b': _L0_ffn_in['expert_b'], 'L0_c': _L0_c, 'L0_wmod': _L0_wmod}
    _x0 = _d['L0_attn_x']
    _d['L0_attn_x'] = jax.random.normal(jax.random.fold_in(jax.random.key(seed), 1), (4, 256, 512), dtype=_x0.dtype)
    del _x0
    return _d

def reference(L0_attn_x, L0_attn_w_qkv, L0_attn_b_qkv, L0_attn_w_o, L0_attn_b_o, L0_ffn_gate_w, L0_ffn_expert_w, L0_ffn_expert_b, L0_c, L0_wmod):

    def _L0_attn_ref(x, w_qkv, b_qkv, w_o, b_o):
        import jax, jax.numpy as jnp
        import numpy as np
        import math
        D_MODEL = 512
        NUM_HEADS = 32
        NUM_KV_HEADS = 8
        HEAD_DIM = D_MODEL // NUM_HEADS
        GROUP = NUM_HEADS // NUM_KV_HEADS
        SEQ_LEN = 256
        BATCH = 2
        ROPE_THETA = 10000.0

        def apply_rope(x, start_pos=0):
            b, h, s, hd = x.shape
            inv_freq = 1.0 / ROPE_THETA ** (jnp.arange(0, hd, 2, dtype=jnp.float32) / hd)
            pos = jnp.arange(start_pos, start_pos + s, dtype=jnp.float32)
            ang = pos[:, None] * inv_freq[None, :]
            cos = jnp.cos(ang).astype(x.dtype)
            sin = jnp.sin(ang).astype(x.dtype)
            xr = x[..., 0::2]
            xi = x[..., 1::2]
            out_r = xr * cos - xi * sin
            out_i = xr * sin + xi * cos
            return jnp.stack([out_r, out_i], axis=-1).reshape(b, h, s, hd)
        bs, seq_len, d_model = x.shape
        qkv = x @ w_qkv.T + b_qkv
        q_dim = NUM_HEADS * HEAD_DIM
        kv_dim = NUM_KV_HEADS * HEAD_DIM
        q, k, v = jnp.split(qkv, [q_dim, q_dim + kv_dim], axis=-1)
        q = q.reshape(bs, seq_len, NUM_HEADS, HEAD_DIM).transpose(0, 2, 1, 3)
        k = k.reshape(bs, seq_len, NUM_KV_HEADS, HEAD_DIM).transpose(0, 2, 1, 3)
        v = v.reshape(bs, seq_len, NUM_KV_HEADS, HEAD_DIM).transpose(0, 2, 1, 3)
        q = apply_rope(q, 0)
        k = apply_rope(k, 0)
        k = jnp.repeat(k, GROUP, axis=1)
        v = jnp.repeat(v, GROUP, axis=1)
        scores = jnp.einsum('bhqd,bhkd->bhqk', q, k) / math.sqrt(HEAD_DIM)
        causal = jnp.tril(jnp.ones((seq_len, seq_len), dtype=bool))
        scores = jnp.where(causal[None, None, :, :], scores, jnp.float32(-1e+20))
        attn = jax.nn.softmax(scores, axis=-1)
        out = jnp.einsum('bhqk,bhkd->bhqd', attn, v)
        out = out.transpose(0, 2, 1, 3).reshape(bs, seq_len, d_model)
        return out @ w_o.T + b_o

    def _L0_ffn_ref(x, gate_w, expert_w, expert_b):
        import jax, jax.numpy as jnp
        import numpy as np
        NUM_EXPERTS = 32
        D_MODEL = 512
        TOP_K = 2
        B, S, D = x.shape
        T = B * S
        xf = x.reshape(T, D)
        logits = xf @ gate_w.T
        w, idx = jax.lax.top_k(logits, TOP_K)
        w = jax.nn.softmax(w, axis=-1)
        combine = jnp.zeros((T, NUM_EXPERTS), dtype=x.dtype).at[jnp.arange(T)[:, None], idx].add(w)

        def body(acc, params):
            W, b, c = params
            return (acc + c[:, None] * (xf @ W.T + b), None)
        out, _ = jax.lax.scan(body, jnp.zeros_like(xf), (expert_w, expert_b, combine.T))
        return out.reshape(B, S, D)
    x = L0_attn_x
    mod = (_silu(L0_c) @ L0_wmod).reshape(L0_c.shape[0], 6, 1, -1)
    sa, ca, ga, sb, cb, gb = (mod[:, 0], mod[:, 1], mod[:, 2], mod[:, 3], mod[:, 4], mod[:, 5])
    ga = (2 * (ga >= 0) - 1) * jnp.maximum(jnp.abs(ga), 0.25)
    gb = (2 * (gb >= 0) - 1) * jnp.maximum(jnp.abs(gb), 0.25)
    h = _layernorm(x, axis=-1) * (1 + ca) + sa
    x = x + ga * _L0_attn_ref(h, L0_attn_w_qkv, L0_attn_b_qkv, L0_attn_w_o, L0_attn_b_o)
    h = _layernorm(x, axis=-1) * (1 + cb) + sb
    x = x + gb * _L0_ffn_ref(h, L0_ffn_gate_w, L0_ffn_expert_w, L0_ffn_expert_b)
    return x

_drawn_inputs = setup_inputs


def setup_inputs(seed=0):
    import zlib

    import numpy as np

    out = dict(_drawn_inputs(seed))
    spreads = {}
    factors = {'L0_attn_b_qkv': 8.0, 'L0_attn_b_o': 8.0, 'L0_ffn_expert_b': 8.0}
    for name, (base, spread) in spreads.items():
        noise = np.random.default_rng([zlib.crc32(name.encode()), seed]).standard_normal(out[name].shape)
        drawn = base * np.exp(spread * noise) if base else spread * noise
        out[name] = jnp.asarray(drawn.astype(out[name].dtype))
    for name, factor in factors.items():
        out[name] = (out[name] * factor).astype(out[name].dtype)
    return out
```

```python
import concourse.bass as bass
from concourse import mybir
from contextlib import ExitStack

F32 = mybir.dt.float32
BF16 = mybir.dt.bfloat16
I32 = mybir.dt.int32
U32 = mybir.dt.uint32
ALU = mybir.AluOpType
ACT = mybir.ActivationFunctionType
AX = mybir.AxisListType

B, S, D = 4, 256, 512
H, KVH, HD = 32, 8, 16
GROUP = H // KVH
E, TOP = 32, 2
P = 128
KT = D // P
QTS = S // P
T = B * QTS
KV = KVH * HD
QKV = D + 2 * KV
EPS = 1e-5
NMOD = 6

ORDER = [0, 2, 4, 6, 1, 3, 5, 7]
STEPS = T * KVH
SPLITS = [(0, 0), (1, 0), (0, 1)]

CAP = P
PRIM = E * CAP
OVB = (B * S * TOP - 1) // CAP
SLOTS = PRIM + OVB * CAP
BIG = 65536.0
RING = 8
KEPT = 4

C_ID, C_MASK, C_TRI, C_IOTA, C_BASE, C_THR, C_J, C_ROPE = 0, 128, 256, 384, 416, 448, 456, 472
C_END = C_ROPE + QTS * 2 * HD


def unit(n, h):
    t, i = divmod(n, KVH)
    return (t // 2) * 3 * KVH + (i if t % 2 == 0 else KVH + 2 * i + h)


def schedule():
    jobs = [("ln1", 0), ("mods", 0), ("hT", 0), ("qkv", 0), ("mods", 1), ("split", 0), ("stack", 0)]
    for n in range(STEPS + 12):
        t, s = divmod(n, KVH)
        if n < STEPS:
            jobs.append(("scores", n))
        if 1 <= n < STEPS + 1:
            jobs.append(("turn", n - 1))
        if n >= 2 and (n - 2) % 4 == 3 and n - 2 < STEPS:
            jobs.append(("pv", (n - 2) // 4))
        for at, job in ((0, "ln1"), (1, "hT"), (2, "qkv"), (4, "split"), (6, "stack")):
            if s == at and t + 1 < T and n < STEPS:
                jobs.append((job, t + 1))
        for at, job in ((2, "norm"), (3, "wo"), (4, "ln2"), (5, "h2T"), (6, "route"), (7, "place")):
            if s == at and 1 <= t <= T:
                jobs.append((job, t - 1))
    return jobs


def bank_uses(jobs):
    uses, n = {}, 0
    fills = {"hT": ["hT"], "qkv": ["q", "kv"], "stack": ["s0", "s1", "s2", "s3", "sk"], "norm": ["rb"],
             "wo": ["wo"], "h2T": ["h2T"], "route": ["gate"], "place": ["rank"]}
    for job, i in jobs:
        for name in ["mcol"] if (job, i) == ("mods", 0) else fills.get(job, []):
            uses[(name, i)] = n
            n += 1
    return uses, n


def program(nc, x, cT, wmod, wqkv, bqkv, wo, bo, gate, ew, eb, const, out):
    JOBS = schedule()
    USES, NUSES = bank_uses(JOBS)

    ctx = ExitStack()
    with ctx:
        def sb(name, shape, dt=F32):
            return ctx.enter_context(nc.sbuf_tensor(name, shape, dt))

        def sem(name):
            return ctx.enter_context(nc.semaphore(name))

        modrow = nc.dram_tensor("modrow", (5, B, D), F32, kind="Internal").ap()
        xs = nc.dram_tensor("xs", (SLOTS, D), F32, kind="Internal").ap()
        ys = nc.dram_tensor("ys", (SLOTS, D), F32, kind="Internal").ap()
        hs = nc.dram_tensor("hs", (T * P, D), F32, kind="Internal").ap()

        ring = sb("ring", [P, RING, KT * D])
        xt = sb("xt", [P, T, D])
        wqkv_sb = sb("wqkv_sb", [P, KT, QKV])
        wo_sb = sb("wo_sb", [P, GROUP, D])
        gate_sb = sb("gate_sb", [P, KT, E])
        bqkv_bc = sb("bqkv_bc", [P, QKV])
        eb_sb = sb("eb_sb", [E, D])
        cst = sb("cst", [P, C_END])
        identB = sb("identB", [P, P], BF16)
        maskB = sb("maskB", [P, P], BF16)
        triB = sb("triB", [P, P], BF16)
        onesB = sb("onesB", [P, P], BF16)
        cT_sb = sb("cT_sb", [P, KT * B])
        sil = sb("sil", [P, 2, KT * B])
        sil8 = sb("sil8", [P, KT, 8, B])
        modcol = sb("modcol", [P, KT, 64])
        bc = sb("bc", [P, 2, 4, D])
        st6 = sb("st6", [P, 2, T, 6])
        mv = sb("mv", [P, 2, T, 2])
        veps = sb("veps", [P, 2, T, 1])
        rstd = sb("rstd", [P, 2, T, 1])
        half = sb("half", [P, 1])
        xh = sb("xh", [P, 2, D])
        hT = sb("hT", [P, 2, KT, P])
        qk = sb("qk", [P, D + KV])
        ra = sb("ra", [P, D + KV])
        rb = sb("rb", [P, D + KV])
        qp = sb("qp", [P, H, 5, HD], BF16)
        kp = sb("kp", [P, KVH, 3, HD], BF16)
        qs = sb("qs", [96, 2, H, P], BF16)
        ks = sb("ks", [96, 2, KVH, S], BF16)
        vz = sb("vz", [P, 2, QTS, KVH, 2 * HD])
        pr = sb("pr", [P, 2, GROUP, S])
        nmax = sb("nmax", [P, 2, KVH, GROUP])
        rsum = sb("rsum", [P, 2, KVH, GROUP])
        rinv = sb("rinv", [P, KVH, GROUP])
        rx = sb("rx", [P, GROUP, KVH * HD])
        rbc = sb("rbc", [P, D])
        aT = sb("aT", [P, GROUP * P])
        xg = rbc
        t2 = sb("t2", [P, D])
        h2 = sb("h2", [P, 2, D])
        hm = sb("hm", [P, D])
        h2T = sb("h2T", [P, KT * P])
        lg = sb("lg", [P, E])
        top = sb("top", [P, T, 8])
        tid = sb("tid", [P, 8], U32)
        tif = sb("tif", [P, 8])
        dlt = sb("dlt", [P, T])
        ex = sb("ex", [P, T])
        e1 = sb("e1", [P, T])
        cw = sb("cw", [P, TOP, T])
        oh = sb("oh", [P, TOP, T, E])
        cnt = sb("cnt", [P, T, E], BF16)
        cum = sb("cum", [P, T + 1, E], BF16)
        pa = sb("pa", [P, 2, E])
        pp = sb("pp", [P, TOP, E])
        pos = sb("pos", [P, TOP, T])
        posi = sb("posi", [P, TOP, T], I32)
        far = sb("far", [P, TOP, T])
        dsel = sb("dsel", [P, TOP, T])
        posg = sb("posg", [P, TOP, T])
        posgi = sb("posgi", [P, TOP, T], I32)
        ovf = sb("ovf", [P, TOP, T])
        ovi = sb("ovi", [P, TOP, T], I32)
        ones = sb("ones", [P, E])
        nb = sb("nb", [P, E])
        inc = sb("inc", [P, E])
        de = sb("de", [P, 3, E])
        ejf = sb("ejf", [P, OVB + 1])
        ctl = sb("ctl", [P, OVB + 1], I32)
        zero = sb("zero", [P, D // 8])

        modA, modB, rowt, bo_bc = hm, h2T, h2, t2
        spare = wqkv_sb[:, :, :].rearrange("p k n -> p (k n)")
        ohd = spare[:, 0:TOP * T * E].rearrange("p (s t e) -> p s t e", s=TOP, t=T)
        nbm = spare[:, 512:768].rearrange("p (e m) -> p e m", e=E)
        ejm = spare[:, 768:1280].rearrange("p (j e) -> p j e", e=E)
        cm = spare[:, 1280:1536].rearrange("p (t e) -> p t e", t=T)
        cmT = spare[0:E, 1536:1792].rearrange("e (s q) -> e s q", s=2)
        xe = xh[:, :, :]
        xeT = hT[:, :, :, :].rearrange("p s k q -> p s (k q)")
        ye = bc[:, 1, 0:2, :]
        yg = pr[:, :, :, :].rearrange("p s j k -> p s (j k)").rearrange("p s (w d) -> p s w d", d=D)

        def bank(name):
            return ctx.enter_context(nc.psum_tensor(name, [P, 512], F32))
        SB = [bank(f"SB{i}") for i in range(3)]
        TB = [bank(f"TB{i}") for i in range(2)]
        OB = bank("OB")
        GB = [bank(f"GB{i}") for i in range(2)]

        ld_x = [sem(f"ld_x{i}") for i in range(2)]
        ld_c = sem("ld_c")
        ld_const = sem("ld_const")
        ld_wqkv = sem("ld_wqkv")
        ld_bias = sem("ld_bias")
        ld_wo = sem("ld_wo")
        ld_gate = sem("ld_gate")
        ld_w = [sem(f"ld_w{i}") for i in range(RING)]
        ld_bc = [sem(f"ld_bc{i}") for i in range(2)]
        ld_gb = sem("ld_gb")
        st_mod = sem("st_mod")
        st_zero = sem("st_zero")
        st_h = [sem(f"st_h{i}") for i in range(2)]
        pool_set = sem("pool_set")
        dve_step = sem("dve_step")
        cast_done = sem("cast_done")
        silu_e = sem("silu_e")
        silu_done = sem("silu_done")
        mod_mm = sem("mod_mm")
        mod_rows = sem("mod_rows")
        modc_done = sem("modc_done")
        g_full = [sem(f"g_full{i}") for i in range(2)]
        stats1 = sem("stats1")
        stats2 = sem("stats2")
        rstd1 = sem("rstd1")
        rstd2 = sem("rstd2")
        xh_done = sem("xh_done")
        hT_done = sem("hT_done")
        qk_done = sem("qk_done")
        v_done = sem("v_done")
        ropeA = sem("ropeA")
        roped = sem("roped")
        part1 = sem("part1")
        part23 = sem("part23")
        stacked = sem("stacked")
        s_full = [sem(f"s_full{i}") for i in range(3)]
        max_done = sem("max_done")
        exp_done = sem("exp_done")
        t_full = [sem(f"t_full{i}") for i in range(2)]
        evac_v = sem("evac_v")
        evac_a = sem("evac_a")
        pv_done = sem("pv_done")
        rinv_done = sem("rinv_done")
        rbc_done = sem("rbc_done")
        aT_done = sem("aT_done")
        xg_done = sem("xg_done")
        att_done = sem("att_done")
        x2_done = sem("x2_done")
        h2_done = sem("h2_done")
        h2T_done = sem("h2T_done")
        lg_done = sem("lg_done")
        cnt_done = sem("cnt_done")
        rank_done = sem("rank_done")
        pos_done = sem("pos_done")
        scat = [sem(f"scat{i}") for i in range(2)]
        tot_ready = sem("tot_ready")
        tot_full = sem("tot_full")
        dlt_done = sem("dlt_done")
        ex_done = sem("ex_done")
        ctl_done = sem("ctl_done")
        cm_done = sem("cm_done")
        cmT_full = sem("cmT_full")
        cmT_done = sem("cmT_done")
        eb_full = sem("eb_full")
        eb_done = sem("eb_done")
        ld_xe = [sem(f"ld_xe{i}") for i in range(2)]
        xT_full = sem("xT_full")
        xT_done = sem("xT_done")
        y_full = sem("y_full")
        y_done = sem("y_done")
        st_y = [sem(f"st_y{i}") for i in range(2)]
        ov_zero = sem("ov_zero")
        ov_h = sem("ov_h")
        ov_scat = sem("ov_scat")
        ov_w = sem("ov_w")
        ov_x = sem("ov_x")
        ov_xT = sem("ov_xT")
        ov_xTd = sem("ov_xTd")
        ov_y = sem("ov_y")
        ov_yd = sem("ov_yd")
        ov_st = sem("ov_st")
        gath = [sem(f"gath{i}") for i in range(2)]
        out_done = sem("out_done")
        st_out = sem("st_out")

        ident = cst[:, C_ID:C_ID + P]
        iota = cst[:, C_IOTA:C_IOTA + E]
        base = cst[:, C_BASE:C_BASE + E]
        rope = cst[:, C_ROPE:C_END].rearrange("p (q s d) -> p q s d", q=QTS, s=2)

        def full(eng, key):
            n = USES[key]
            eng.wait_ge(g_full[n % 2], n // 2 + 1)
            return GB[n % 2]

        def read_signal(key):
            name, i = key
            return {"mcol": (modc_done, 1), "hT": (hT_done, i + 1), "q": (qk_done, 2 * i + 1), "kv": (v_done, i + 1),
                    "s0": (stacked, 5 * i + 1), "s1": (stacked, 5 * i + 2), "s2": (stacked, 5 * i + 3),
                    "s3": (stacked, 5 * i + 4), "sk": (stacked, 5 * i + 5), "rb": (rbc_done, i + 1),
                    "wo": (att_done, i + 1), "h2T": (h2T_done, i + 1), "gate": (lg_done, i + 1),
                    "rank": (rank_done, i + 1)}[name]

        KEYS = {n: key for key, n in USES.items()}

        def on_scalar(n, k):
            return (n // KVH) % 2 == 1 and (2 * n + k) % 4 == 3

        def copies(u):
            a = [on_scalar(n, k) for n in range(STEPS) for k in range(1 + (n // KVH) % 2)][:u]
            return len(a) - sum(a), sum(a)

        def p_turned(n, k):
            c = n % 4
            at = (2 * (c % 2) + k) * 512
            return ring[:, KEPT + 2 * (n // 4 % 2) + c // 2, at:at + 512]

        block = ctx.enter_context(nc.Block())

        @block.sync
        def _(sp):
            def load_mod(m):
                sp.dma_start(ring[:, m, :], wmod[m]).then_inc(ld_w[m], 16)

            sp.dma_start(cT_sb[:, :], cT).then_inc(ld_c, 16)
            for i in range(2):
                sp.dma_start(xt[:, i, :], x[i * P:(i + 1) * P, :]).then_inc(ld_x[i], 16)
            sp.dma_start(cst[:, :], const).then_inc(ld_const, 16)
            for m in range(2):
                load_mod(m)
            sp.dma_start(wqkv_sb[:, :, :], wqkv).then_inc(ld_wqkv, 16)
            sp.dma_start(bqkv_bc[:, :], bqkv.partition_broadcast(P)).then_inc(ld_bias, 16)
            sp.dma_start(bo_bc[:, :], bo.partition_broadcast(P)).then_inc(ld_bias, 16)
            for m in range(2, NMOD):
                load_mod(m)
            sp.wait_ge(ld_x[0], 16)
            sp.dma_start(xt[:, 2:T, :], x[2 * P:, :].rearrange("(t p) d -> p t d", p=P)).then_inc(ld_x[0], 16)
            sp.dma_start(wo_sb[:, :, :], wo).then_inc(ld_wo, 16)
            sp.dma_start(gate_sb[:, :, :], gate).then_inc(ld_gate, 16)
            sp.dma_start(eb_sb[:, :], eb).then_inc(ld_gate, 16)
            sp.wait_ge(mod_rows, 2)
            sp.dma_start(modrow[0], modA[64:64 + B, :]).then_inc(st_mod, 16)
            sp.dma_start(modrow[1], rowt[64:64 + B, 0, :]).then_inc(st_mod, 16)
            sp.dma_start(modrow[2], modB[0:B, :]).then_inc(st_mod, 16)
            sp.dma_start(modrow[3], modA[96:96 + B, :]).then_inc(st_mod, 16)
            sp.dma_start(modrow[4], modB[32:32 + B, :]).then_inc(st_mod, 16)
            sp.wait_ge(st_mod, 80)
            for b in range(2):
                sp.dma_start(bc[:, b, :, :], modrow[0:4, b, :].partition_broadcast(P)).then_inc(ld_bc[b], 16)
            sp.wait_ge(mod_mm, 2)
            for e in range(KEPT):
                sp.dma_start(ring[:, e, :], ew[e]).then_inc(ld_w[e], 16)
            sp.wait_ge(pool_set, 5)
            for e in range(E):
                sp.dma_start(xs[e * CAP:(e + 1) * CAP, :].rearrange("p (w d) -> p w d", w=8), zero[:, :].unsqueeze(1).to_broadcast([P, 8, D // 8])).then_inc(st_zero, 16)
            for j in range(OVB):
                sp.dma_start(ys[PRIM + j * CAP:PRIM + (j + 1) * CAP, :].rearrange("p (w d) -> p w d", w=8),
                             zero[:, :].unsqueeze(1).to_broadcast([P, 8, D // 8])).then_inc(st_zero, 16)
            for t in range(T):
                sp.wait_ge(h2_done, t + 1)
                sp.dma_start(hs[t * P:(t + 1) * P, :], h2[:, t % 2, :]).then_inc(st_h[t % 2], 16)
                if t % 2 == 1 and t < T - 1:
                    b = t // 2 + 2
                    if b < B:
                        sp.dma_start(bc[:, b % 2, :, :], modrow[0:4, b, :].partition_broadcast(P)).then_inc(ld_bc[b % 2], 16)
                    elif b == B:
                        sp.dma_start(bc[:, 0, :, :], modrow[4].partition_broadcast(P)).then_inc(ld_gb, 16)
                if t == T - 2:
                    sp.wait_ge(pv_done, STEPS // 4)
                    for e in range(KEPT, RING):
                        sp.dma_start(ring[:, e, :], ew[e]).then_inc(ld_w[e], 16)
            for i in range(2):
                sp.wait_ge(scat[i], 16 * TOP * T // 2)
            for e in range(E):
                if e >= 2:
                    sp.wait_ge(xT_full, e - 1)
                sp.dma_start(xe[:, e % 2, :], xs[e * CAP:(e + 1) * CAP, :]).then_inc(ld_xe[e % 2], 16)
                if e >= 2 and e - 2 + RING < E:
                    sp.wait_ge(y_full, e - 1)
                    sp.dma_start(ring[:, (e - 2) % RING, :], ew[e - 2 + RING]).then_inc(ld_w[(e - 2) % RING], 16)
            sp.wait_ge(ctl_done, 1)
            more = sp.value_load(ctl[0:1, OVB:OVB + 1], min_val=0, max_val=OVB)
            with sp.If(more > 0):
                for j in range(OVB):
                    sp.dma_start(xs[PRIM + j * CAP:PRIM + (j + 1) * CAP, :].rearrange("p (w d) -> p w d", w=8), zero[:, :].unsqueeze(1).to_broadcast([P, 8, D // 8])).then_inc(ov_zero, 16)
                for i in range(2):
                    sp.wait_ge(st_h[i], 16 * T // 2)
                for t in range(T):
                    if t >= 1:
                        sp.wait_ge(ov_scat, 16 * TOP * t)
                    sp.dma_start(h2[:, 0, :], hs[t * P:(t + 1) * P, :]).then_inc(ov_h, 16)
                sp.wait_ge(ov_scat, 16 * TOP * T)
                sp.wait_ge(y_full, E)
                for j in range(OVB):
                    if j >= 1:
                        sp.wait_ge(ov_y, j)
                    of = sp.value_load(ctl[0:1, j:j + 1], min_val=0, max_val=E - 1)
                    sp.dma_start(ring[:, 0:1, :], ew[bass.ds(of, 1), :, :].rearrange("e p n -> p e n")).then_inc(ov_w, 16)
                    sp.dma_start(xe[:, 0, :], xs[PRIM + j * CAP:PRIM + (j + 1) * CAP, :]).then_inc(ov_x, 16)
            for t in range(T):
                sp.wait_ge(out_done, t + 1)
                sp.dma_start(out[t * P:(t + 1) * P, :], xt[:, t, :]).then_inc(st_out, 16)
            sp.wait_ge(st_out, 16 * T)
            for i in range(2):
                sp.wait_ge(st_h[i], 16 * T // 2)

        @block.tensor
        def _(pe):
            def fill(key):
                n = USES[key]
                if n >= 2:
                    signal, count = read_signal(KEYS[n - 2])
                    pe.wait_ge(signal, count)
                return GB[n % 2]

            def filled(ins, key):
                ins.then_inc(g_full[USES[key] % 2], 1)

            def modulation(ms):
                for m in ms:
                    pe.wait_ge(ld_w[m], 16)
                for k in range(KT):
                    for m in ms:
                        at = 32 * (m % 4)
                        mm = pe.matmul(TB[m // 4][at:at + 32, :],
                                       sil8[:, k, :, :].rearrange("p r b -> p (r b)"),
                                       ring[:, m, k * D:(k + 1) * D], start=(k == 0), stop=(k == KT - 1))
                mm.then_inc(mod_mm, 1)

            pe.wait_ge(ld_const, 16)
            for job, i in JOBS:
                if job == "mods" and i == 0:
                    pe.wait_ge(silu_done, 1)
                    modulation([0, 1])
                    bk = fill(("mcol", 0))
                    pe.wait_ge(mod_rows, 1)
                    for k in range(KT):
                        mm = pe.transpose(bk[:, k * 64:(k + 1) * 64], modA[0:64, k * P:(k + 1) * P], cst[0:64, C_ID:C_ID + 64])
                    filled(mm, ("mcol", 0))
                elif job == "mods":
                    modulation(range(2, NMOD))
                elif job == "hT":
                    bk = fill(("hT", i))
                    pe.wait_ge(xh_done, i + 1)
                    for k in range(KT):
                        mm = pe.transpose(bk[:, k * P:(k + 1) * P], xh[:, i % 2, k * P:(k + 1) * P], ident)
                    filled(mm, ("hT", i))
                elif job == "qkv":
                    bk = fill(("q", i))
                    pe.wait_ge(hT_done, i + 1)
                    if i == 0:
                        pe.wait_ge(ld_wqkv, 16)
                    for k in range(KT):
                        mm = pe.matmul(bk[:, :], hT[:, i % 2, k, :], wqkv_sb[:, k, 0:D], start=(k == 0), stop=(k == KT - 1))
                    filled(mm, ("q", i))
                    bk = fill(("kv", i))
                    for k in range(KT):
                        mm = pe.matmul(bk[:, 0:2 * KV], hT[:, i % 2, k, :], wqkv_sb[:, k, D:QKV],
                                       start=(k == 0), stop=(k == KT - 1))
                    filled(mm, ("kv", i))
                elif job == "stack":
                    pe.wait_ge(part1, i + 1)
                    pe.wait_ge(part23, i + 1)
                    if i == 0:
                        pe.wait_ge(cast_done, 1)
                    for c in range(5):
                        key = (f"s{c}" if c < 4 else "sk", i)
                        rows = fill(key)[:, :].bitcast(BF16)
                        for u in range(8):
                            h = 8 * c + u
                            src, firsts = (qp[:, h, :, :], (0, 2, 3)) if c < 4 else (kp[:, u, :, :], (1, 1, 0))
                            for r, at in enumerate(firsts):
                                mm = pe.transpose(rows[32 * r:32 * r + 32, u * P:(u + 1) * P],
                                                  src[:, at:at + 2, :].rearrange("p w d -> p (w d)"), identB[:, :])
                        filled(mm, key)
                elif job == "scores":
                    t, s = divmod(i, KVH)
                    g, qt, b = ORDER[s], t % 2, t // 2
                    if s == 0:
                        pe.wait_ge(stacked, 5 * (t + 1))
                    heads, keys = GROUP // (1 + qt), P * (1 + qt)
                    for hh in range(1 + qt):
                        u = unit(i, hh)
                        if u >= 3:
                            pe.wait_ge(exp_done, u - 2)
                        sc = SB[u % 3][:, :].rearrange("p (h k) -> p h k", k=keys)
                        pe.matmul(sc[:, :, keys - P:keys], identB[:, :], maskB[:, :].unsqueeze(1).to_broadcast([P, heads, P]),
                                  start=True, stop=False, skip_group_check=True)
                        for j in range(heads):
                            mm = pe.matmul(sc[:, j, :], qs[:, t % 2, GROUP * g + hh * heads + j, :], ks[:, b % 2, g, 0:keys],
                                           start=False, stop=(j == heads - 1), skip_group_check=True)
                        mm.then_inc(s_full[u % 3], 1)
                elif job == "turn":
                    qt = i // KVH % 2
                    pe.wait_ge(exp_done, unit(i, qt) + 1)
                    for k in range(1 + qt):
                        u = unit(i, k)
                        v, a = copies(u - 1) if u >= 2 else (0, 0)
                        if v:
                            pe.wait_ge(evac_v, v)
                        if a:
                            pe.wait_ge(evac_a, a)
                        if u < 2:
                            pe.wait_ge(mod_rows, 2)
                        for j in range(GROUP):
                            mm = pe.transpose(TB[u % 2][:, j * P:(j + 1) * P], pr[:, i % 2, j, k * P:(k + 1) * P], ident)
                        mm.then_inc(t_full[u % 2], 1)
                elif job == "pv":
                    t, qd = divmod(i, 2)
                    qt, b = t % 2, t // 2
                    v, a = copies(unit(4 * i + 3, qt) + 1)
                    pe.wait_ge(evac_v, v)
                    if a:
                        pe.wait_ge(evac_a, a)
                    if qd == 0:
                        pe.wait_ge(v_done, t + 1)
                        if t >= 1:
                            pe.wait_ge(aT_done, t)
                    for k in range(1 + qt):
                        for c in range(4):
                            g = ORDER[4 * qd + c]
                            at = 32 * (g // 2)
                            mm = pe.matmul(OB[at:at + 32, :], vz[:, b % 2, k, g, :], p_turned(4 * i + c, k),
                                           start=(qd == 0 and k == 0), stop=(qd == 1 and k == qt), skip_group_check=True)
                    mm.then_inc(pv_done, 1)
                elif job == "norm":
                    bk = fill(("rb", i))
                    pe.wait_ge(rinv_done, i + 1)
                    for j in range(GROUP):
                        mm = pe.transpose(bk[:, j * P:(j + 1) * P], rx[:, j, :], ident)
                    filled(mm, ("rb", i))
                elif job == "wo":
                    bk = fill(("wo", i))
                    pe.wait_ge(aT_done, i + 1)
                    if i == 0:
                        pe.wait_ge(ld_wo, 16)
                    for j in range(GROUP):
                        mm = pe.matmul(bk[:, :], aT[:, j * P:(j + 1) * P], wo_sb[:, j, :], start=(j == 0), stop=(j == GROUP - 1))
                    filled(mm, ("wo", i))
                elif job == "h2T":
                    bk = fill(("h2T", i))
                    pe.wait_ge(h2_done, i + 1)
                    for k in range(KT):
                        mm = pe.transpose(bk[:, k * P:(k + 1) * P], h2[:, i % 2, k * P:(k + 1) * P], ident)
                    filled(mm, ("h2T", i))
                elif job == "route":
                    bk = fill(("gate", i))
                    pe.wait_ge(h2T_done, i + 1)
                    if i == 0:
                        pe.wait_ge(ld_gate, 32)
                    for k in range(KT):
                        mm = pe.matmul(bk[:, 0:E], h2T[:, k * P:(k + 1) * P], gate_sb[:, k, :], start=(k == 0), stop=(k == KT - 1))
                    filled(mm, ("gate", i))
                elif job == "place":
                    bk = fill(("rank", i))
                    pe.wait_ge(cnt_done, i + 1)
                    pe.matmul(bk[:, 0:E], triB[:, :], cnt[:, i, :], start=True, stop=False)
                    mm = pe.matmul(bk[:, 0:E], onesB[:, :], cum[:, i, :], start=False, stop=True)
                    filled(mm, ("rank", i))

            def bias_rows(t):
                pe.wait_ge(cmT_done, t + 1)
                if t >= 2:
                    pe.wait_ge(eb_done, t - 1)
                pe.matmul(GB[t % 2][:, :], cmT[:, t % 2, :], eb_sb[:, :], start=True, stop=True).then_inc(eb_full, 1)

            pe.wait_ge(rank_done, T)
            pe.wait_ge(aT_done, T)
            pe.wait_ge(tot_ready, 1)
            pe.matmul(OB[:, 0:E], onesB[:, :], cum[:, T, :], start=True, stop=True).then_inc(tot_full, 1)
            pe.wait_ge(cm_done, 1)
            v, a = copies(3 * KVH * B)
            pe.wait_ge(evac_v, v)
            pe.wait_ge(evac_a, a)
            for t in range(T):
                if t >= 2:
                    pe.wait_ge(cmT_done, t - 1)
                pe.transpose(TB[t % 2][0:E, 0:P], cm[:, t, :], ident).then_inc(cmT_full, 1)
                if t >= 1:
                    bias_rows(t - 1)
            bias_rows(T - 1)
            for e in range(E + 1):
                if e < E:
                    pe.wait_ge(ld_xe[e % 2], 16 * (e // 2 + 1))
                    if e >= 2:
                        pe.wait_ge(xT_done, e - 1)
                    if e == 0:
                        pe.wait_ge(cmT_done, T)
                    for k in range(KT):
                        mm = pe.transpose(TB[e % 2][:, k * P:(k + 1) * P], xe[:, e % 2, k * P:(k + 1) * P], ident)
                    mm.then_inc(xT_full, 1)
                if e >= 1:
                    f = e - 1
                    r = f % RING
                    pe.wait_ge(ld_w[r], 16 * (f // RING + 1 + (r < NMOD)))
                    pe.wait_ge(xT_done, f + 1)
                    if f >= 2:
                        pe.wait_ge(y_done, f - 1)
                    if f == 0:
                        pe.wait_ge(eb_done, T)
                    for k in range(KT):
                        mm = pe.matmul(GB[f % 2][:, :], xeT[:, f % 2, k * P:(k + 1) * P], ring[:, r, k * D:(k + 1) * D],
                                       start=(k == 0), stop=(k == KT - 1))
                    mm.then_inc(y_full, 1)
            pe.wait_ge(ctl_done, 1)
            more = pe.value_load(ctl[0:1, OVB:OVB + 1], min_val=0, max_val=OVB)
            with pe.If(more > 0):
                pe.wait_ge(y_done, E)
                for j in range(OVB):
                    pe.wait_ge(ov_x, 16 * (j + 1))
                    for k in range(KT):
                        mm = pe.transpose(TB[0][:, k * P:(k + 1) * P], xe[:, 0, k * P:(k + 1) * P], ident)
                    mm.then_inc(ov_xT, 1)
                    pe.wait_ge(ov_w, 16 * (j + 1))
                    pe.wait_ge(ov_xTd, j + 1)
                    if j >= 1:
                        pe.wait_ge(ov_yd, j)
                    for k in range(KT):
                        mm = pe.matmul(GB[0][:, :], xeT[:, 0, k * P:(k + 1) * P], ring[:, 0, k * D:(k + 1) * D],
                                       start=(k == 0), stop=(k == KT - 1))
                    mm.then_inc(ov_y, 1)

        @block.scalar
        def _(act):
            act.wait_ge(ld_c, 16)
            act.activation(sil[:, 0, :], cT_sb[:, :], ACT.Exp, scale=-1.0).then_inc(silu_e, 1)
            for job, i in JOBS:
                if job == "hT":
                    b = i // 2
                    bk = full(act, ("hT", i))
                    act.wait_ge(modc_done, 1)
                    if i >= 2:
                        full(act, ("kv", i - 2))
                    for k in range(KT):
                        ins = act.activation(hT[:, i % 2, k, :], bk[:, k * P:(k + 1) * P], ACT.Identity,
                                             bias=modcol[:, k, b:b + 1], scale=modcol[:, k, 32 + b:33 + b])
                    ins.then_inc(hT_done, 1)
                elif job == "split":
                    act.wait_ge(roped, i + 1)
                    if i >= 1:
                        full(act, ("sk", i - 1))
                    act.activation(qp[:, :, 2:4, :], rb[:, 0:D].rearrange("p (h o d) -> p h o d", o=1, d=HD).to_broadcast([P, H, 2, HD]),
                                   ACT.Copy)
                    act.activation(kp[:, :, 1, :], rb[:, D:D + KV].rearrange("p (h d) -> p h d", d=HD), ACT.Copy).then_inc(part1, 1)
                elif job == "scores":
                    t, s = divmod(i, KVH)
                    g, qt = ORDER[s], t % 2
                    heads, keys = GROUP // (1 + qt), P * (1 + qt)
                    if i >= 2:
                        u = unit(i - 2, (i - 2) // KVH % 2)
                        act.wait_ge(t_full[u % 2], u // 2 + 1)
                    for hh in range(1 + qt):
                        u = unit(i, hh)
                        act.wait_ge(max_done, u + 1)
                        sc = SB[u % 3][:, :].rearrange("p (h k) -> p h k", k=keys)
                        for j in range(heads):
                            h = hh * heads + j
                            ins = act.activation(pr[:, i % 2, h, 0:keys], sc[:, j, :], ACT.Exp,
                                                 bias=nmax[:, t % 2, g, h:h + 1], accum_out=rsum[:, t % 2, g, h:h + 1])
                        ins.then_inc(exp_done, 1)
                elif job == "turn":
                    for k in range(1 + i // KVH % 2):
                        if on_scalar(i, k):
                            u = unit(i, k)
                            act.wait_ge(t_full[u % 2], u // 2 + 1)
                            if i // 4 >= 2:
                                act.wait_ge(pv_done, i // 4 - 1)
                            act.activation(p_turned(i, k), TB[u % 2][:, :], ACT.Copy).then_inc(evac_a, 1)
                elif job == "norm":
                    bk = full(act, ("rb", i))
                    if i >= 1:
                        act.wait_ge(x2_done, i)
                    act.activation(rbc[:, :], bk[:, :], ACT.Copy).then_inc(rbc_done, 1)
                elif job == "h2T":
                    bk = full(act, ("h2T", i))
                    if i >= 1:
                        full(act, ("gate", i - 1))
                    act.activation(h2T[:, :], bk[:, :], ACT.Copy).then_inc(h2T_done, 1)
            act.wait_ge(dlt_done, 1)
            act.activation(ex[:, :], dlt[:, :], ACT.Exp).then_inc(ex_done, 1)
            for t in range(T):
                act.wait_ge(cmT_full, t + 1)
                if t >= 2:
                    act.wait_ge(eb_full, t - 1)
                act.activation(cmT[:, t % 2, :], TB[t % 2][0:E, 0:P], ACT.Copy).then_inc(cmT_done, 1)
            for e in range(E + 1):
                if e < E:
                    act.wait_ge(xT_full, e + 1)
                    if e >= 2:
                        act.wait_ge(y_full, e - 1)
                    act.activation(xeT[:, e % 2, :], TB[e % 2][:, :], ACT.Copy).then_inc(xT_done, 1)
                if e >= 1:
                    act.wait_ge(y_done, e)
                    act.dma_start(ys[(e - 1) * CAP:e * CAP, :], ye[:, (e - 1) % 2, :]).then_inc(st_y[(e - 1) % 2], 16)
            act.wait_ge(ctl_done, 1)
            more = act.value_load(ctl[0:1, OVB:OVB + 1], min_val=0, max_val=OVB)
            with act.If(more > 0):
                for j in range(OVB):
                    act.wait_ge(ov_xT, j + 1)
                    if j >= 1:
                        act.wait_ge(ov_y, j)
                    act.activation(xeT[:, 0, :], TB[0][:, :], ACT.Copy).then_inc(ov_xTd, 1)
                    act.wait_ge(ov_yd, j + 1)
                    act.dma_start(ys[PRIM + j * CAP:PRIM + (j + 1) * CAP, :], ye[:, 0, :]).then_inc(ov_st, 16)

        @block.gpsimd
        def _(pool):
            pool.memset(half[:, :], -0.5).then_inc(pool_set, 1)
            pool.memset(vz[:, :, :, :, :].rearrange("p b q g c -> p (b q g c)"), 0.0).then_inc(pool_set, 1)
            pool.memset(onesB[:, :], 1.0).then_inc(pool_set, 1)
            pool.memset(cum[:, 0, :], 0.0).then_inc(pool_set, 1)
            pool.memset(zero[:, :], 0.0).then_inc(pool_set, 1)
            pool.memset(ones[:, :], 1.0).then_inc(pool_set, 1)
            pool.wait_ge(pool_set, 6)
            for job, i in JOBS:
                if job == "ln1":
                    pool.wait_ge(stats1, i + 1)
                    pool.tensor_tensor(rstd[:, 0, i, :], veps[:, 0, i, :], half[:, :], ALU.pow).then_inc(rstd1, 1)
                elif job == "qkv":
                    pool.wait_ge(qk_done, 2 * (i + 1))
                    if i >= 1:
                        pool.wait_ge(roped, i)
                    pool.tensor_tensor(ra[:, :].rearrange("p (h d) -> p h d", d=HD),
                                       qk[:, :].rearrange("p (h d) -> p h d", d=HD),
                                       rope[:, i % 2, 0:1, :].to_broadcast([P, H + KVH, HD]), ALU.mult).then_inc(ropeA, 1)
                elif job == "wo":
                    if i % 2 == 0:
                        pool.wait_ge(ld_bc[i // 2 % 2], 16 * (i // 4 + 1))
                    pool.wait_ge(aT_done, i + 1)
                    pool.tensor_tensor(xg[:, :], xt[:, i, :], bc[:, i // 2 % 2, 1, :], ALU.add).then_inc(xg_done, 1)
                elif job == "ln2":
                    pool.wait_ge(stats2, i + 1)
                    pool.tensor_tensor(rstd[:, 1, i, :], veps[:, 1, i, :], half[:, :], ALU.pow).then_inc(rstd2, 1)
                elif job == "place":
                    pool.wait_ge(pos_done, i + 1)
                    if i == 0:
                        pool.wait_ge(st_zero, 16 * (E + OVB))
                    for s in range(TOP):
                        pool.indirect_dma_start(out=xs[0:PRIM, :], in_=h2[:, i % 2, :], in_offset=None,
                                                out_offset=bass.IndirectOffsetOnAxis(ap=posi[:, s, i:i + 1], axis=0),
                                                bounds_check=PRIM - 1, oob_is_err=False).then_inc(scat[i % 2], 16)
            pool.wait_ge(ctl_done, 1)
            more = pool.value_load(ctl[0:1, OVB:OVB + 1], min_val=0, max_val=OVB)
            with pool.If(more > 0):
                pool.wait_ge(ov_zero, 16 * OVB)
                for t in range(T):
                    pool.wait_ge(ov_h, 16 * (t + 1))
                    for s in range(TOP):
                        pool.indirect_dma_start(out=xs, in_=h2[:, 0, :], in_offset=None,
                                                out_offset=bass.IndirectOffsetOnAxis(ap=ovi[:, s, t:t + 1], axis=0),
                                                bounds_check=SLOTS - 1, oob_is_err=False).then_inc(ov_scat, 16)
                pool.wait_ge(ov_st, 16 * OVB)
            for i in range(2):
                pool.wait_ge(st_y[i], 16 * E // 2)
            for t in range(T):
                if t >= 2:
                    pool.wait_ge(out_done, t - 1)
                for s in range(TOP):
                    pool.indirect_dma_start(out=yg[:, t % 2, s, :], out_offset=None, in_=ys,
                                            in_offset=bass.IndirectOffsetOnAxis(ap=posgi[:, s, t:t + 1], axis=0),
                                            bounds_check=SLOTS - 1, oob_is_err=False).then_inc(gath[t % 2], 16)

        @block.vector
        def _(dve):
            taken = [0]

            def step(ins):
                taken[0] += 1
                ins.then_inc(dve_step, 1)
                dve.wait_ge(dve_step, taken[0])

            def statistics(ln, i, done):
                step(dve.bn_stats(st6[:, ln, i, :], xt[:, i, :]))
                step(dve.bn_aggr(mv[:, ln, i, :], st6[:, ln, i, :]))
                dve.tensor_scalar(veps[:, ln, i, :], mv[:, ln, i, 1:2], EPS, None, ALU.add).then_inc(done, 1)

            def gate_rows(src, rows, out_rows):
                dve.tensor_scalar(rowt[rows, 1, :], src, 0.0, 2.0, ALU.is_ge, ALU.mult)
                step(dve.tensor_scalar(rowt[rows, 0, :], src, -1.0, 0.25, ALU.mult, ALU.max))
                step(dve.tensor_tensor(rowt[rows, 0, :], rowt[rows, 0, :], src, ALU.max))
                step(dve.scalar_tensor_tensor(out=out_rows, in0=rowt[rows, 1, :], scalar=-1.0, in1=rowt[rows, 0, :],
                                              op0=ALU.add, op1=ALU.mult))

            dve.wait_ge(silu_e, 1)
            step(dve.tensor_scalar(sil[:, 1, :], sil[:, 0, :], 1.0, None, ALU.add))
            step(dve.reciprocal(sil[:, 0, :], sil[:, 1, :]))
            rows = [v.rearrange("p (k b) -> p k b", b=B).unsqueeze(2).to_broadcast([P, KT, 8, B]) for v in (sil[:, 0, :], cT_sb[:, :])]
            dve.tensor_tensor(sil8[:, :, :, :], rows[0], rows[1], ALU.mult).then_inc(silu_done, 1)
            dve.wait_ge(ld_const, 16)
            dve.tensor_copy(identB[:, :], cst[:, C_ID:C_ID + P])
            dve.tensor_copy(maskB[:, :], cst[:, C_MASK:C_MASK + P])
            dve.tensor_copy(triB[:, :], cst[:, C_TRI:C_TRI + P]).then_inc(cast_done, 1)

            for job, i in JOBS:
                if job == "mods" and i == 0:
                    dve.wait_ge(mod_mm, 1)
                    dve.tensor_copy(modA[0:32, :], TB[0][0:32, :])
                    dve.tensor_scalar(modA[32:64, :], TB[0][32:64, :], 1.0, None, ALU.add).then_inc(mod_rows, 1)
                    bk = full(dve, ("mcol", 0))
                    dve.tensor_copy(modcol[:, :, :], bk[:, 0:KT * 64].rearrange("p (k m) -> p k m", k=KT)).then_inc(modc_done, 1)
                elif job == "mods":
                    dve.wait_ge(mod_mm, 2)
                    dve.wait_ge(ld_bias, 32)
                    gate_rows(TB[0][64:96, :], slice(64, 96), modA[64:96, :])
                    dve.tensor_tensor(rowt[64:96, 0, :], modA[64:96, :], bo_bc[64:96, :], ALU.mult)
                    dve.tensor_copy(modA[96:128, :], TB[0][96:128, :])
                    dve.tensor_scalar(modB[0:32, :], TB[1][0:32, :], 1.0, None, ALU.add)
                    gate_rows(TB[1][32:64, :], slice(32, 64), modB[32:64, :])
                    dve.tensor_copy(ejf[:, 0:1], cst[:, 0:1]).then_inc(mod_rows, 1)
                elif job == "ln1":
                    dve.wait_ge(ld_x[min(i, 1)] if i < 2 else ld_x[0], 16 if i < 2 else 32)
                    statistics(0, i, stats1)
                    dve.wait_ge(rstd1, i + 1)
                    if i >= 2:
                        full(dve, ("hT", i - 2))
                    dve.tensor_scalar(xh[:, i % 2, :], xt[:, i, :], mv[:, 0, i, 0:1], rstd[:, 0, i, :],
                                      ALU.subtract, ALU.mult).then_inc(xh_done, 1)
                elif job == "qkv":
                    b, qt = i // 2, i % 2
                    bk = full(dve, ("q", i))
                    if i == 0:
                        dve.wait_ge(ld_bias, 32)
                        dve.wait_ge(pool_set, 6)
                    dve.tensor_tensor(qk[:, 0:D], bk[:, :], bqkv_bc[:, 0:D], ALU.add).then_inc(qk_done, 1)
                    bk = full(dve, ("kv", i))
                    dve.tensor_tensor(qk[:, D:D + KV], bk[:, 0:KV], bqkv_bc[:, D:D + KV], ALU.add).then_inc(qk_done, 1)
                    vp = vz[:, b % 2, qt, :, :].rearrange("p g c -> p (g c)").rearrange("p (a w d) -> p a w d", w=4, d=HD)
                    dve.tensor_tensor(vp[:, :, 0:4:3, :], bk[:, KV:2 * KV].rearrange("p (a w d) -> p a w d", w=2, d=HD),
                                      bqkv_bc[:, D + KV:QKV].rearrange("p (a w d) -> p a w d", w=2, d=HD),
                                      ALU.add).then_inc(v_done, 1)
                    dve.wait_ge(qk_done, 2 * (i + 1))
                    if i >= 1:
                        dve.wait_ge(part23, i)
                    pairs = qk[:, :].rearrange("p (h d two) -> p h d two", h=H + KVH, two=2)
                    sin = rope[:, qt, 1:2, :].rearrange("p o (d two) -> p o d two", two=2)
                    turned = rb[:, :].rearrange("p (h d two) -> p h d two", h=H + KVH, two=2)
                    for w in range(2):
                        ins = dve.tensor_tensor(turned[:, :, :, w], pairs[:, :, :, 1 - w],
                                                sin[:, :, :, w].to_broadcast([P, H + KVH, HD // 2]), ALU.mult)
                    step(ins)
                    dve.wait_ge(ropeA, i + 1)
                    dve.tensor_tensor(rb[:, :], rb[:, :], ra[:, :], ALU.add).then_inc(roped, 1)
                elif job == "split":
                    dve.wait_ge(roped, i + 1)
                    dve.wait_ge(part1, i + 1)
                    if i >= 1:
                        full(dve, ("sk", i - 1))
                    rq = rb[:, 0:D].rearrange("p (h d) -> p h d", d=HD)
                    rk = rb[:, D:D + KV].rearrange("p (h d) -> p h d", d=HD)
                    dve.tensor_tensor(rq, rq, qp[:, :, 2, :], ALU.subtract)
                    step(dve.tensor_tensor(rk, rk, kp[:, :, 1, :], ALU.subtract))
                    dve.tensor_copy(qp[:, :, 0:2, :], rq.unsqueeze(2).to_broadcast([P, H, 2, HD]))
                    step(dve.tensor_copy(kp[:, :, 2, :], rk))
                    dve.tensor_tensor(qp[:, :, 4, :], rq, qp[:, :, 0, :], ALU.subtract)
                    dve.tensor_tensor(kp[:, :, 0, :], rk, kp[:, :, 2, :], ALU.subtract).then_inc(part23, 1)
                elif job == "stack":
                    for c in range(4):
                        rows = full(dve, (f"s{c}", i))[0:96, :].bitcast(BF16)
                        dve.tensor_copy(qs[:, i % 2, 8 * c:8 * c + 8, :].rearrange("p h q -> p (h q)"), rows).then_inc(stacked, 1)
                    rows = full(dve, ("sk", i))[0:96, :].bitcast(BF16)
                    dve.tensor_copy(ks[:, i // 2 % 2, :, (i % 2) * P:(i % 2 + 1) * P],
                                    rows.rearrange("p (g q) -> p g q", g=KVH)).then_inc(stacked, 1)
                elif job == "scores":
                    t, s = divmod(i, KVH)
                    g, qt = ORDER[s], t % 2
                    heads, keys = GROUP // (1 + qt), P * (1 + qt)
                    for hh in range(1 + qt):
                        u = unit(i, hh)
                        dve.wait_ge(s_full[u % 3], u // 3 + 1)
                        dve.tensor_reduce(nmax[:, t % 2, g, hh * heads:(hh + 1) * heads],
                                          SB[u % 3][:, :].rearrange("p (h k) -> p h k", k=keys), AX.X, ALU.max,
                                          negate=True).then_inc(max_done, 1)
                elif job == "turn":
                    for k in range(1 + i // KVH % 2):
                        if not on_scalar(i, k):
                            u = unit(i, k)
                            dve.wait_ge(t_full[u % 2], u // 2 + 1)
                            if i // 4 >= 2:
                                dve.wait_ge(pv_done, i // 4 - 1)
                            dve.tensor_copy(p_turned(i, k), TB[u % 2][:, :]).then_inc(evac_v, 1)
                elif job == "norm":
                    t = i
                    dve.wait_ge(exp_done, unit(KVH * t + KVH - 1, t % 2) + 1)
                    if i >= 1:
                        full(dve, ("rb", i - 1))
                    step(dve.reciprocal(rinv[:, :, :], rsum[:, t % 2, :, :]))
                    for j in range(GROUP):
                        ins = dve.tensor_copy(rx[:, j, :].rearrange("p (g d) -> p g d", d=HD),
                                              rinv[:, :, j:j + 1].to_broadcast([P, KVH, HD]))
                    ins.then_inc(rinv_done, 1)
                elif job == "wo":
                    dve.wait_ge(rbc_done, i + 1)
                    dve.wait_ge(pv_done, 2 * (i + 1))
                    if i >= 1:
                        full(dve, ("wo", i - 1))
                    dve.tensor_tensor(aT[:, :], OB[:, :], rbc[:, :], ALU.mult).then_inc(aT_done, 1)
                    if i % 2 == 0:
                        dve.wait_ge(ld_bc[i // 2 % 2], 16 * (i // 4 + 1))
                    bk = full(dve, ("wo", i))
                    dve.tensor_tensor(t2[:, :], bk[:, :], bc[:, i // 2 % 2, 0, :], ALU.mult).then_inc(att_done, 1)
                    dve.wait_ge(att_done, i + 1)
                    dve.wait_ge(xg_done, i + 1)
                    dve.tensor_tensor(xt[:, i, :], t2[:, :], xg[:, :], ALU.add).then_inc(x2_done, 1)
                elif job == "ln2":
                    dve.wait_ge(x2_done, i + 1)
                    statistics(1, i, stats2)
                    step(dve.scalar_tensor_tensor(out=hm[:, :], in0=xt[:, i, :], scalar=mv[:, 1, i, 0:1],
                                                  in1=bc[:, i // 2 % 2, 2, :], op0=ALU.subtract, op1=ALU.mult))
                    dve.wait_ge(rstd2, i + 1)
                    if i >= 2:
                        dve.wait_ge(scat[i % 2], 16 * TOP * (i // 2))
                        dve.wait_ge(st_h[i % 2], 16 * (i // 2))
                        full(dve, ("h2T", i - 2))
                    dve.scalar_tensor_tensor(out=h2[:, i % 2, :], in0=hm[:, :], scalar=rstd[:, 1, i, :],
                                             in1=bc[:, i // 2 % 2, 3, :], op0=ALU.mult, op1=ALU.add).then_inc(h2_done, 1)
                elif job == "route":
                    bk = full(dve, ("gate", i))
                    dve.tensor_copy(lg[:, :], bk[:, 0:E]).then_inc(lg_done, 1)
                    dve.wait_ge(lg_done, i + 1)
                    step(dve.max(top[:, i, :], lg[:, :]))
                    step(dve.max_index(tid[:, :], top[:, i, :], lg[:, :]))
                    step(dve.tensor_copy(tif[:, :], tid[:, :]))
                    for s in range(TOP):
                        ins = dve.tensor_scalar(oh[:, s, i, :], iota, tif[:, s:s + 1], None, ALU.is_equal)
                    step(ins)
                    dve.tensor_tensor(cnt[:, i, :], oh[:, 0, i, :], oh[:, 1, i, :], ALU.add).then_inc(cnt_done, 1)
                    dve.wait_ge(cnt_done, i + 1)
                    ins = dve.tensor_tensor(cum[:, i + 1, :], cum[:, i, :], cnt[:, i, :], ALU.add)
                    if i == T - 1:
                        ins.then_inc(tot_ready, 1)
                    else:
                        step(ins)
                elif job == "place":
                    bk = full(dve, ("rank", i))
                    dve.tensor_scalar(pa[:, 0, :], bk[:, 0:E], float(CAP), BIG, ALU.is_ge, ALU.mult)
                    dve.tensor_tensor(pa[:, 1, :], bk[:, 0:E], base, ALU.add).then_inc(rank_done, 1)
                    dve.wait_ge(rank_done, i + 1)
                    step(dve.tensor_tensor(pa[:, 0, :], pa[:, 0, :], pa[:, 1, :], ALU.add))
                    step(dve.tensor_tensor(pp[:, :, :], oh[:, :, i, :], pa[:, 0:1, :].to_broadcast([P, TOP, E]), ALU.mult))
                    step(dve.tensor_reduce(pos[:, :, i], pp[:, :, :], AX.X, ALU.add))
                    dve.tensor_copy(posi[:, :, i], pos[:, :, i]).then_inc(pos_done, 1)

            dve.tensor_tensor(dlt[:, :], top[:, :, 1], top[:, :, 0], ALU.subtract).then_inc(dlt_done, 1)
            dve.wait_ge(ex_done, 1)
            step(dve.tensor_scalar(e1[:, :], ex[:, :], 1.0, None, ALU.add))
            step(dve.reciprocal(cw[:, 0, :], e1[:, :]))
            step(dve.tensor_tensor(cw[:, 1, :], ex[:, :], cw[:, 0, :], ALU.mult))
            for s in range(TOP):
                ins = dve.tensor_tensor(ohd[:, s, :, :], oh[:, s, :, :], cw[:, s, :].unsqueeze(2).to_broadcast([P, T, E]), ALU.mult)
            step(ins)
            dve.tensor_tensor(cm[:, :, :], ohd[:, 0, :, :], ohd[:, 1, :, :], ALU.add).then_inc(cm_done, 1)
            dve.wait_ge(cm_done, 1)

            dve.wait_ge(tot_full, 1)
            step(dve.tensor_tensor(nbm[:, :, :], OB[:, 0:E].unsqueeze(2).to_broadcast([P, E, 8]),
                                   cst[:, C_THR:C_THR + 8].unsqueeze(1).to_broadcast([P, E, 8]), ALU.is_gt))
            step(dve.tensor_reduce(nb[:, :], nbm[:, :, :], AX.X, ALU.add))
            step(dve.tensor_tensor_scan(inc[:, :], ones[:, :], nb[:, :], 0.0, ALU.mult, ALU.add))
            step(dve.tensor_tensor(de[:, 0, :], inc[:, :], nb[:, :], ALU.subtract))
            step(dve.tensor_scalar(de[:, 1, :], de[:, 0, :], float(CAP), PRIM - CAP - BIG, ALU.mult, ALU.add))
            step(dve.tensor_tensor(de[:, 2, :], de[:, 1, :], base, ALU.subtract))
            for s in range(TOP):
                ins = dve.tensor_tensor(ohd[:, s, :, :], oh[:, s, :, :], de[:, 2:3, :].to_broadcast([P, T, E]), ALU.mult)
            step(ins)
            dve.tensor_scalar(far[:, :, :], pos[:, :, :], BIG, None, ALU.is_ge)
            step(dve.tensor_reduce(dsel[:, :, :], ohd[:, :, :, :], AX.X, ALU.add))
            step(dve.tensor_tensor(dsel[:, :, :], dsel[:, :, :], far[:, :, :], ALU.mult))
            dve.tensor_scalar(ovf[:, :, :], far[:, :, :], -BIG, BIG, ALU.mult, ALU.add)
            step(dve.tensor_tensor(posg[:, :, :], pos[:, :, :], dsel[:, :, :], ALU.add))
            step(dve.tensor_tensor(ovf[:, :, :], ovf[:, :, :], posg[:, :, :], ALU.add))
            dve.tensor_copy(posgi[:, :, :], posg[:, :, :])
            dve.tensor_copy(ovi[:, :, :], ovf[:, :, :])
            step(dve.tensor_tensor(ejm[:, :, :], inc[:, :].unsqueeze(1).to_broadcast([P, OVB + 1, E]),
                                   cst[:, C_J:C_J + OVB + 1].unsqueeze(2).to_broadcast([P, OVB + 1, E]), ALU.is_le))
            step(dve.tensor_reduce(ejf[:, :], ejm[:, :, :], AX.X, ALU.add))
            step(dve.tensor_copy(ejf[:, OVB:OVB + 1], inc[:, E - 1:E]))
            dve.tensor_scalar(ctl[:, :], ejf[:, :], float(E - 1), None, ALU.min).then_inc(ctl_done, 1)

            dve.wait_ge(ld_gb, 16)
            for t in range(T):
                dve.wait_ge(eb_full, t + 1)
                dve.tensor_tensor(t2[:, :], GB[t % 2][:, :], bc[:, 0, t // 2, :], ALU.mult).then_inc(eb_done, 1)
                dve.wait_ge(eb_done, t + 1)
                step(dve.tensor_tensor(xt[:, t, :], xt[:, t, :], t2[:, :], ALU.add))
            for e in range(E):
                dve.wait_ge(y_full, e + 1)
                if e >= 2:
                    dve.wait_ge(st_y[e % 2], 16 * (e // 2))
                dve.tensor_copy(ye[:, e % 2, :], GB[e % 2][:, :]).then_inc(y_done, 1)
            more = dve.value_load(ctl[0:1, OVB:OVB + 1], min_val=0, max_val=OVB)
            with dve.If(more > 0):
                for i in range(2):
                    dve.wait_ge(st_y[i], 16 * E // 2)
                for j in range(OVB):
                    dve.wait_ge(ov_y, j + 1)
                    if j >= 1:
                        dve.wait_ge(ov_st, 16 * j)
                    dve.tensor_copy(ye[:, 0, :], GB[0][:, :]).then_inc(ov_yd, 1)
            for t in range(T):
                ya, yb = yg[:, t % 2, 0, :], yg[:, t % 2, 1, :]
                dve.wait_ge(gath[t % 2], 16 * TOP * (t // 2 + 1))
                step(dve.tensor_scalar(ya, ya, cw[:, 0, t:t + 1], None, ALU.mult))
                step(dve.scalar_tensor_tensor(out=yb, in0=yb, scalar=cw[:, 1, t:t + 1], in1=ya, op0=ALU.mult, op1=ALU.add))
                step(dve.tensor_tensor(yb, yb, bc[:, 0, t // 2, :], ALU.mult))
                dve.tensor_tensor(xt[:, t, :], xt[:, t, :], yb, ALU.add).then_inc(out_done, 1)


def constants():
    import numpy as np
    c = np.zeros((P, C_END), np.float32)
    r = np.arange(P)
    c[:, C_ID:C_ID + P] = np.eye(P)
    c[:, C_MASK:C_MASK + P] = np.where(r[None, :] <= r[:, None], 0.0, -1e20)
    c[:, C_TRI:C_TRI + P] = r[:, None] < r[None, :]
    c[:, C_IOTA:C_IOTA + E] = np.arange(E)
    c[:, C_BASE:C_BASE + E] = np.arange(E) * CAP
    c[:, C_THR:C_THR + 8] = np.arange(1, 9) * CAP
    c[:, C_J:C_J + OVB + 1] = np.arange(OVB + 1)
    inv = (1.0 / np.float32(10000.0) ** (np.arange(0, HD, 2, dtype=np.float32) / np.float32(HD))).astype(np.float32)
    angle = np.arange(S, dtype=np.float32)[:, None] * inv[None, :]
    cos, sin = 0.5 * np.cos(angle), 0.5 * np.sin(angle)
    table = np.stack([np.stack([cos, cos], -1).reshape(S, HD), np.stack([-sin, sin], -1).reshape(S, HD)], 1)
    c[:, C_ROPE:C_END] = table.reshape(QTS, P, 2, HD).transpose(1, 0, 2, 3).reshape(P, -1)
    return c


def kernel(**inputs):
    import numpy as np
    import concourse.bacc as bacc
    from concourse.bass_utils import run_bass_kernel_spmd

    a = {k: np.asarray(v) for k, v in inputs.items()}
    arrays = {
        "x": a["L0_attn_x"].reshape(B * S, D),
        "cT": a["L0_c"].T.reshape(KT, P, B).transpose(1, 0, 2).reshape(P, KT * B),
        "wmod": a["L0_wmod"].reshape(KT, P, NMOD, D).transpose(2, 1, 0, 3).reshape(NMOD, P, KT * D),
        "wqkv": a["L0_attn_w_qkv"].T.reshape(KT, P, QKV).transpose(1, 0, 2),
        "bqkv": a["L0_attn_b_qkv"],
        "wo": a["L0_attn_w_o"].T.reshape(KVH, GROUP, HD, D).transpose(0, 2, 1, 3).reshape(P, GROUP, D),
        "bo": a["L0_attn_b_o"],
        "gate": a["L0_ffn_gate_w"].T.reshape(KT, P, E).transpose(1, 0, 2),
        "ew": a["L0_ffn_expert_w"].transpose(0, 2, 1).reshape(E, KT, P, D).transpose(0, 2, 1, 3).reshape(E, P, KT * D),
        "eb": a["L0_ffn_expert_b"],
        "const": constants(),
    }
    arrays = {f"in_{k}": np.ascontiguousarray(v) for k, v in arrays.items()}
    nc = bacc.Bacc("TRN2", target_bir_lowering=False, num_devices=1)
    args = [nc.dram_tensor(k, v.shape, mybir.dt.from_np(v.dtype), kind="ExternalInput").ap() for k, v in arrays.items()]
    out = nc.dram_tensor("out", (B * S, D), F32, kind="ExternalOutput").ap()
    program(nc, *args, out)
    r = run_bass_kernel_spmd(nc, [arrays], core_ids=[0])
    return r.results[0]["out"].reshape(B, S, D)
```

```python
import concourse.bass as bass
from concourse import mybir
from contextlib import ExitStack

F32 = mybir.dt.float32
BF16 = mybir.dt.bfloat16
I32 = mybir.dt.int32
U32 = mybir.dt.uint32
ALU = mybir.AluOpType
ACT = mybir.ActivationFunctionType
AX = mybir.AxisListType

B, S, D = 4, 256, 512
H, KVH, HD = 32, 8, 16
GROUP = H // KVH
E, TOP = 32, 2
P = 128
KT = D // P
QTS = S // P
T = B * QTS
KV = KVH * HD
QKV = D + 2 * KV
EPS = 1e-5
NMOD = 6

ORDER = [0, 2, 4, 6, 1, 3, 5, 7]
STEPS = T * KVH
SPLITS = [(0, 0), (1, 0), (0, 1)]

CAP = 96
PRIM = E * CAP
STRIP = 32
TILES = PRIM // P
OVB = (B * S * TOP - 1) // CAP
MOST = (B * S - 1) // CAP
SLOTS = PRIM + OVB * CAP
BIG = 65536.0
RING = 8
KEPT = 4

C_ID, C_MASK, C_TRI, C_IOTA, C_BASE, C_THR = 0, P, 2 * P, 3 * P, 3 * P + E, 3 * P + 2 * E
C_J = C_THR + MOST
C_MOD = C_J + OVB + 1
C_ROPE = C_MOD + 1
C_END = C_ROPE + QTS * 2 * HD


def unit(n, h):
    t, i = divmod(n, KVH)
    return (t // 2) * 3 * KVH + (i if t % 2 == 0 else KVH + 2 * i + h)



def expert(i, c):
    return (i * P + c * STRIP) // CAP


def last_tile(e):
    return ((e + 1) * CAP - 1) // P


WHEN = {'ln1': -19.5, 'xh': -18.7, 'hT': -17.4, 'qkv': -15.5, 'bias': -15.4, 'rope': -14.7, 'split': -12.9, 'rest': -12.3, 'stack0': -10.7, 'stack1': -10.69, 'stack2': -10.68, 'stack3': -9.9, 'stack4': -9.59, 'parts': -1.8, 'peaks': -1.4, 'sums': 10.2, 'norm': 11.2, 'wo': 14.2, 'x2': 14.7, 'ln2': 15.2, 'h2': 17.1, 'h2T': 19.0, 'route': 19.1, 'choose': 21.0, 'place': 23.2, 'pos': 24.4}
LEAD = 8.9
LAG = 1.2
EARLY = 4.5
MODS = -11.0


def schedule():
    jobs = [(-18, "mods", 0), (MODS, "mods", 1)]
    for t in range(T):
        jobs += [(KVH * t + at - EARLY * (t == 1 and at < WHEN["rope"]), name[:5] if name[:5] == "stack" else name, 5 * t + int(name[5]) if name[:5] == "stack" else t)
                 for name, at in WHEN.items()]
    jobs += [(n, "probs", n) for n in range(STEPS)]
    jobs += [(n - LEAD, "peak", n) for n in range(STEPS)]
    jobs += [(4 * i + 3 + LAG, "pv", i) for i in range(STEPS // 4)]
    return [(name, i) for _, name, i in sorted(jobs)]


def bank_uses(jobs):
    uses, n = {}, 0
    fills = {"hT": ["hT"], "qkv": ["q", "kv"], "stack": ["stack"], "peaks": ["peaks"], "wo": ["wo"], "h2T": ["h2T"], "route": ["gate"], "place": ["rank"]}
    for job, i in jobs:
        for name in ["mcol"] if (job, i) == ("mods", 0) else fills.get(job, []):
            uses[(name, i)] = n
            n += 1
    return uses, n


def program(nc, x, cT, wmod, wqkv, bqkv, wo, bo, gate, ew, eb, const, out):
    JOBS = schedule()
    USES, NUSES = bank_uses(JOBS)

    ctx = ExitStack()
    with ctx:
        def sb(name, shape, dt=F32):
            return ctx.enter_context(nc.sbuf_tensor(name, shape, dt))

        def sem(name):
            return ctx.enter_context(nc.semaphore(name))

        modrow = nc.dram_tensor("modrow", (5, B, D), F32, kind="Internal").ap()
        xs = nc.dram_tensor("xs", (SLOTS, D), F32, kind="Internal").ap()
        ys = nc.dram_tensor("ys", (SLOTS, D), F32, kind="Internal").ap()
        hs = nc.dram_tensor("hs", (T * P, D), F32, kind="Internal").ap()

        ring = sb("ring", [P, RING, KT * D])
        xt = sb("xt", [P, T, D])
        wqkv_sb = sb("wqkv_sb", [P, KT, QKV])
        wo_sb = sb("wo_sb", [P, GROUP, D])
        gate_sb = sb("gate_sb", [P, KT, E])
        bqkv_bc = sb("bqkv_bc", [P, QKV])
        eb_sb = sb("eb_sb", [3 * E, D])
        cst = sb("cst", [P, C_END])
        identB = sb("identB", [P, P], BF16)
        maskB = sb("maskB", [P, P], BF16)
        triB = sb("triB", [P, P], BF16)
        onesB = sb("onesB", [P, P], BF16)
        cT_sb = sb("cT_sb", [P, KT * B])
        sil = sb("sil", [P, 2, KT * B])
        sil8 = sb("sil8", [P, KT, 8, B])
        modcol = sb("modcol", [P, KT, 64])
        bc = sb("bc", [P, 2, 4, D])
        st6 = sb("st6", [P, 2, T, 6])
        mv = sb("mv", [P, 2, T, 2])
        veps = sb("veps", [P, 2, T, 1])
        rstd = sb("rstd", [P, 2, T, 1])
        half = sb("half", [P, 1])
        xh = sb("xh", [P, 2, D])
        hT = sb("hT", [P, 2, KT, P])
        qk = sb("qk", [P, D + KV])
        ra = sb("ra", [P, D + KV])
        rb = sb("rb", [P, D + KV])
        qp = sb("qp", [P, H, 5, HD], BF16)
        kp = sb("kp", [P, KVH, 3, HD], BF16)
        qs = sb("qs", [96, 3, H, P], BF16)
        ks = sb("ks", [96, 2, KVH, S], BF16)
        vone = sb("vone", [P, 2, QTS, KVH, 2, HD])
        nmax = sb("nmax", [P, 2, KVH, GROUP])
        nrem = sb("nrem", [P, 2, H])
        npart = sb("npart", [P, 3, H], BF16)
        nT = sb("nT", [96, 2, P], BF16)
        pick = sb("pick", [96, H], BF16)
        opick = sb("opick", [96, OVB], BF16)
        pvT = sb("pvT", [P, 2, 16, 2, HD])
        zinv = sb("zinv", [P, 2, 16])
        aT = sb("aT", [P, GROUP * P])
        xg = sb("xg", [P, D])
        t2 = pvT[:, 1, :, :, :].rearrange("p b w d -> p (b w d)")
        h2 = sb("h2", [P, 2, D])
        hm = sb("hm", [P, D])
        h2T = sb("h2T", [P, KT * P])
        lg = sb("lg", [P, E])
        top = sb("top", [P, T, 8])
        tid = sb("tid", [P, 8], U32)
        tif = sb("tif", [P, 8])
        dlt = sb("dlt", [P, T])
        ex = sb("ex", [P, T])
        e1 = sb("e1", [P, T])
        cw = sb("cw", [P, TOP, T])
        oh = sb("oh", [P, TOP, T, E])
        cnt = sb("cnt", [P, T, E], BF16)
        cum = sb("cum", [P, T + 1, E], BF16)
        pa = sb("pa", [P, 2, E])
        pp = sb("pp", [P, TOP, E])
        pos = sb("pos", [P, TOP, T])
        posi = sb("posi", [P, TOP, T], I32)
        far = sb("far", [P, TOP, T])
        dsel = sb("dsel", [P, TOP, T])
        posg = sb("posg", [P, TOP, T])
        posgi = sb("posgi", [P, TOP, T], I32)
        ovf = sb("ovf", [P, TOP, T])
        ovi = sb("ovi", [P, TOP, T], I32)
        ones = sb("ones", [P, E])
        nb = sb("nb", [P, E])
        inc = sb("inc", [P, E])
        de = sb("de", [P, 3, E])
        ejf = sb("ejf", [P, OVB + 1])
        ctl = sb("ctl", [P, OVB + 1], I32)
        zero = sb("zero", [P, D // 8])

        modA, modB, rowt, bo_bc = hm, h2T, h2, xg
        spare = wqkv_sb[:, :, :].rearrange("p k n -> p (k n)")
        ohd = spare[:, 0:TOP * T * E].rearrange("p (s t e) -> p s t e", s=TOP, t=T)
        nbm = spare[:, 512:832].rearrange("p (e m) -> p e m", e=E)
        ejm = spare[:, 832:1536].rearrange("p (j e) -> p j e", e=E)
        ebp = spare[0:3 * E, 1792:2048].bitcast(BF16)
        xe = [xh[:, 0, :], xh[:, 1, :], ra[:, 0:D], rb[:, 0:D]]
        xeT = hT[:, :, :, :].rearrange("p s k q -> p s (k q)")
        ye = [bc[:, 1, i, :] for i in range(4)]
        yg = [[xg[:, :], aT[:, :]], [h2T[:, :], hm[:, :]], [ra[:, 0:D], rb[:, 0:D]], [qk[:, 0:D], t2]]

        def bank(name):
            return ctx.enter_context(nc.psum_tensor(name, [P, 512], F32))
        SB = [bank(f"SB{i}") for i in range(2)]
        TB = [bank(f"TB{i}") for i in range(2)]
        OB = [bank(f"OB{i}") for i in range(2)]
        GB = [bank(f"GB{i}") for i in range(2)]

        ld_x = [sem(f"ld_x{i}") for i in range(2)]
        ld_c = sem("ld_c")
        ld_const = sem("ld_const")
        ld_wqkv = sem("ld_wqkv")
        ld_bias = sem("ld_bias")
        ld_wo = sem("ld_wo")
        ld_gate = sem("ld_gate")
        ld_w = [sem(f"ld_w{i}") for i in range(RING)]
        ld_bc = [sem(f"ld_bc{i}") for i in range(2)]
        ld_gb = sem("ld_gb")
        st_mod = sem("st_mod")
        st_zero = sem("st_zero")
        st_h = [sem(f"st_h{i}") for i in range(2)]
        pool_set = sem("pool_set")
        dve_step = sem("dve_step")
        cast_done = sem("cast_done")
        silu_e = sem("silu_e")
        silu_done = sem("silu_done")
        mod_mm = sem("mod_mm")
        mod_rows = sem("mod_rows")
        modc_done = sem("modc_done")
        g_full = [sem(f"g_full{i}") for i in range(2)]
        stats1 = sem("stats1")
        stats2 = sem("stats2")
        rstd1 = sem("rstd1")
        rstd2 = sem("rstd2")
        xh_done = sem("xh_done")
        hT_done = sem("hT_done")
        qk_done = sem("qk_done")
        v_done = sem("v_done")
        ropeA = sem("ropeA")
        roped = sem("roped")
        part1 = sem("part1")
        rest1 = sem("rest1")
        part2 = sem("part2")
        part3 = sem("part3")
        stacked = sem("stacked")
        s_full = [sem(f"s_full{i}") for i in range(2)]
        max_done = sem("max_done")
        npart_done = sem("npart_done")
        nT_done = sem("nT_done")
        t_full = [sem(f"t_full{i}") for i in range(2)]
        exp_done = sem("exp_done")
        causal = sem("causal")
        pv_done = sem("pv_done")
        pv_read = sem("pv_read")
        aT_done = sem("aT_done")
        xg_done = sem("xg_done")
        att_done = sem("att_done")
        x2_done = sem("x2_done")
        h2_done = sem("h2_done")
        h2T_done = sem("h2T_done")
        lg_done = sem("lg_done")
        cnt_done = sem("cnt_done")
        rank_done = sem("rank_done")
        pos_done = sem("pos_done")
        scat = [sem(f"scat{i}") for i in range(2)]
        tot_ready = sem("tot_ready")
        tot_full = sem("tot_full")
        dlt_done = sem("dlt_done")
        ex_done = sem("ex_done")
        ctl_done = sem("ctl_done")
        ebp_done = sem("ebp_done")
        ya_done = sem("ya_done")
        ld_xe = [sem(f"ld_xe{i}") for i in range(4)]
        xT_full = sem("xT_full")
        xT_done = sem("xT_done")
        y_full = sem("y_full")
        y_done = sem("y_done")
        st_y = [sem(f"st_y{i}") for i in range(4)]
        ov_zero = sem("ov_zero")
        ov_h = sem("ov_h")
        ov_scat = sem("ov_scat")
        ov_w = sem("ov_w")
        ov_x = sem("ov_x")
        ov_xT = sem("ov_xT")
        ov_xTd = sem("ov_xTd")
        ov_y = sem("ov_y")
        ov_yd = sem("ov_yd")
        ov_st = sem("ov_st")
        gath = [sem(f"gath{i}") for i in range(4)]
        out_done = sem("out_done")
        st_out = sem("st_out")

        ident = cst[:, C_ID:C_ID + P]
        iota = cst[:, C_IOTA:C_IOTA + E]
        base = cst[:, C_BASE:C_BASE + E]
        rope = cst[:, C_ROPE:C_END].rearrange("p (q s d) -> p q s d", q=QTS, s=2)

        def full(eng, key):
            n = USES[key]
            eng.wait_ge(g_full[n % 2], n // 2 + 1)
            return GB[n % 2]

        def read_signal(key):
            name, i = key
            return {"mcol": (modc_done, 1), "hT": (hT_done, i + 1), "q": (qk_done, 2 * i + 1), "kv": (v_done, i + 1),
                    "stack": (stacked, i + 1), "peaks": (nT_done, i + 1),
                    "wo": (att_done, i + 1), "h2T": (h2T_done, i + 1), "gate": (lg_done, i + 1),
                    "rank": (rank_done, i + 1)}[name]

        KEYS = {n: key for key, n in USES.items()}

        def p_turned(n, k):
            c = n % 4
            at = (2 * (c % 2) + k) * 512
            return ring[:, KEPT + 2 * (n // 4 % 2) + c // 2, at:at + 512]

        block = ctx.enter_context(nc.Block())

        @block.sync
        def _(sp):
            def load_mod(m):
                sp.dma_start(ring[:, m, :], wmod[m]).then_inc(ld_w[m], 16)

            sp.dma_start(cT_sb[:, :], cT).then_inc(ld_c, 16)
            for i in range(2):
                sp.dma_start(xt[:, i, :], x[i * P:(i + 1) * P, :]).then_inc(ld_x[i], 16)
            sp.dma_start(cst[:, :], const).then_inc(ld_const, 16)
            for m in range(2):
                load_mod(m)
            sp.dma_start(wqkv_sb[:, :, :], wqkv).then_inc(ld_wqkv, 16)
            sp.dma_start(bqkv_bc[:, :], bqkv.partition_broadcast(P)).then_inc(ld_bias, 16)
            sp.dma_start(bo_bc[:, :], bo.partition_broadcast(P)).then_inc(ld_bias, 16)
            for m in range(2, NMOD):
                load_mod(m)
            sp.wait_ge(ld_x[0], 16)
            sp.dma_start(xt[:, 2:T, :], x[2 * P:, :].rearrange("(t p) d -> p t d", p=P)).then_inc(ld_x[0], 16)
            sp.dma_start(wo_sb[:, :, :], wo).then_inc(ld_wo, 16)
            sp.dma_start(gate_sb[:, :, :], gate).then_inc(ld_gate, 16)
            for w in range(3):
                sp.dma_start(eb_sb[32 * w:32 * (w + 1), :], eb).then_inc(ld_gate, 16)
            sp.wait_ge(mod_rows, 2)
            sp.dma_start(modrow[0], modA[64:64 + B, :]).then_inc(st_mod, 16)
            sp.dma_start(modrow[1], rowt[64:64 + B, 0, :]).then_inc(st_mod, 16)
            sp.dma_start(modrow[2], modB[0:B, :]).then_inc(st_mod, 16)
            sp.dma_start(modrow[3], modA[96:96 + B, :]).then_inc(st_mod, 16)
            sp.dma_start(modrow[4], modB[32:32 + B, :]).then_inc(st_mod, 16)
            sp.wait_ge(st_mod, 80)
            for b in range(2):
                sp.dma_start(bc[:, b, :, :], modrow[0:4, b, :].partition_broadcast(P)).then_inc(ld_bc[b], 16)
            sp.wait_ge(mod_mm, 2)
            for e in range(KEPT):
                sp.dma_start(ring[:, e, :], ew[e]).then_inc(ld_w[e], 16)
            sp.wait_ge(pool_set, 5)
            for e in range(TILES):
                sp.dma_start(xs[e * P:(e + 1) * P, :].rearrange("p (w d) -> p w d", w=8), zero[:, :].unsqueeze(1).to_broadcast([P, 8, D // 8])).then_inc(st_zero, 16)
            for j in range(OVB):
                sp.dma_start(ys[PRIM + j * CAP:PRIM + (j + 1) * CAP, :].rearrange("p (w d) -> p w d", w=8),
                             zero[0:CAP, :].unsqueeze(1).to_broadcast([CAP, 8, D // 8])).then_inc(st_zero, 16)
            for t in range(T):
                sp.wait_ge(h2_done, t + 1)
                sp.dma_start(hs[t * P:(t + 1) * P, :], h2[:, t % 2, :]).then_inc(st_h[t % 2], 16)
                if t % 2 == 1 and t < T - 1:
                    b = t // 2 + 2
                    if b < B:
                        sp.dma_start(bc[:, b % 2, :, :], modrow[0:4, b, :].partition_broadcast(P)).then_inc(ld_bc[b % 2], 16)
                    elif b == B:
                        sp.dma_start(bc[:, 0, :, :], modrow[4].partition_broadcast(P)).then_inc(ld_gb, 16)
                if t == T - 2:
                    sp.wait_ge(pv_done, STEPS // 4)
                    for e in range(KEPT, RING):
                        sp.dma_start(ring[:, e, :], ew[e]).then_inc(ld_w[e], 16)
            for i in range(2):
                sp.wait_ge(scat[i], 16 * TOP * T // 2)
            for i in range(4):
                sp.dma_start(xe[i], xs[i * P:(i + 1) * P, :]).then_inc(ld_xe[i], 16)
            for i in range(TILES):
                if i + 4 < TILES:
                    sp.wait_ge(xT_full, i + 1)
                    sp.dma_start(xe[i % 4], xs[(i + 4) * P:(i + 5) * P, :]).then_inc(ld_xe[i % 4], 16)
                for e in range(E - RING):
                    if last_tile(e) == i:
                        sp.wait_ge(y_full, i + 1)
                        sp.dma_start(ring[:, e % RING, :], ew[e + RING]).then_inc(ld_w[e % RING], 16)
            sp.wait_ge(ctl_done, 1)
            more = sp.value_load(ctl[0:1, OVB:OVB + 1], min_val=0, max_val=OVB)
            with sp.If(more > 0):
                for j in range(OVB):
                    sp.dma_start(xs[PRIM + j * CAP:PRIM + (j + 1) * CAP, :].rearrange("p (w d) -> p w d", w=8), zero[0:CAP, :].unsqueeze(1).to_broadcast([CAP, 8, D // 8])).then_inc(ov_zero, 16)
                for i in range(2):
                    sp.wait_ge(st_h[i], 16 * T // 2)
                for t in range(T):
                    if t >= 1:
                        sp.wait_ge(ov_scat, 16 * TOP * t)
                    sp.dma_start(h2[:, 0, :], hs[t * P:(t + 1) * P, :]).then_inc(ov_h, 16)
                sp.wait_ge(ov_scat, 16 * TOP * T)
                sp.wait_ge(y_full, TILES)
                for j in range(OVB):
                    if j >= 1:
                        sp.wait_ge(ov_y, j)
                    of = sp.value_load(ctl[0:1, j:j + 1], min_val=0, max_val=E - 1)
                    sp.dma_start(ring[:, 0:1, :], ew[bass.ds(of, 1), :, :].rearrange("e p n -> p e n")).then_inc(ov_w, 16)
                    sp.dma_start(xe[0][0:CAP, :], xs[PRIM + j * CAP:PRIM + (j + 1) * CAP, :]).then_inc(ov_x, 16)
            for t in range(T):
                sp.wait_ge(out_done, t + 1)
                sp.dma_start(out[t * P:(t + 1) * P, :], xt[:, t, :]).then_inc(st_out, 16)
            sp.wait_ge(st_out, 16 * T)
            for i in range(2):
                sp.wait_ge(st_h[i], 16 * T // 2)

        @block.tensor
        def _(pe):
            def fill(key):
                n = USES[key]
                if n >= 2:
                    signal, count = read_signal(KEYS[n - 2])
                    pe.wait_ge(signal, count)
                return GB[n % 2]

            def filled(ins, key):
                ins.then_inc(g_full[USES[key] % 2], 1)

            def modulation(ms):
                for m in ms:
                    pe.wait_ge(ld_w[m], 16)
                for k in range(KT):
                    for m in ms:
                        at = 32 * (m % 4)
                        mm = pe.matmul(TB[m // 4][at:at + 32, :],
                                       sil8[:, k, :, :].rearrange("p r b -> p (r b)"),
                                       ring[:, m, k * D:(k + 1) * D], start=(k == 0), stop=(k == KT - 1))
                mm.then_inc(mod_mm, 1)

            pe.wait_ge(ld_const, 16)
            pe.wait_ge(cast_done, 1)
            for job, i in JOBS:
                if job == "mods" and i == 0:
                    pe.wait_ge(silu_done, 1)
                    modulation([0, 1])
                    bk = fill(("mcol", 0))
                    pe.wait_ge(mod_rows, 1)
                    for k in range(KT):
                        mm = pe.transpose(bk[:, k * 64:(k + 1) * 64], modA[0:64, k * P:(k + 1) * P], cst[0:64, C_ID:C_ID + 64])
                    filled(mm, ("mcol", 0))
                elif job == "mods":
                    modulation(range(2, NMOD))
                elif job == "hT":
                    bk = fill(("hT", i))
                    pe.wait_ge(xh_done, i + 1)
                    for k in range(KT):
                        mm = pe.transpose(bk[:, k * P:(k + 1) * P], xh[:, i % 2, k * P:(k + 1) * P], ident)
                    filled(mm, ("hT", i))
                elif job == "qkv":
                    bk = fill(("q", i))
                    pe.wait_ge(hT_done, i + 1)
                    if i == 0:
                        pe.wait_ge(ld_wqkv, 16)
                    for k in range(KT):
                        mm = pe.matmul(bk[:, :], hT[:, i % 2, k, :], wqkv_sb[:, k, 0:D], start=(k == 0), stop=(k == KT - 1))
                    filled(mm, ("q", i))
                    bk = fill(("kv", i))
                    for k in range(KT):
                        mm = pe.matmul(bk[:, 0:2 * KV], hT[:, i % 2, k, :], wqkv_sb[:, k, D:QKV],
                                       start=(k == 0), stop=(k == KT - 1))
                    filled(mm, ("kv", i))
                elif job == "stack":
                    t, c = divmod(i, 5)
                    pe.wait_ge(part1, t + 1)
                    pe.wait_ge(part2, t + 1)
                    pe.wait_ge(part3, t + 1)
                    rows = fill((job, i))[:, :].bitcast(BF16)
                    for u in range(8):
                        h = 8 * c + u
                        src, firsts = (qp[:, h, :, :], (0, 2, 3)) if c < 4 else (kp[:, u, :, :], (1, 1, 0))
                        for r, at in enumerate(firsts):
                            mm = pe.transpose(rows[32 * r:32 * r + 32, u * P:(u + 1) * P],
                                              src[:, at:at + 2, :].rearrange("p w d -> p (w d)"), identB[:, :])
                    filled(mm, (job, i))
                elif job == "peak":
                    t, s = divmod(i, KVH)
                    g, qt, b = ORDER[s], t % 2, t // 2
                    if s == 0:
                        pe.wait_ge(stacked, 5 * (t + 1))
                    heads, keys = GROUP // (1 + qt), P * (1 + qt)
                    for hh in range(1 + qt):
                        u = unit(i, hh)
                        if u >= 2:
                            pe.wait_ge(max_done, u - 1)
                        sc = SB[u % 2][:, :].rearrange("p (h k) -> p h k", k=keys)
                        pe.matmul(sc[:, :, keys - P:keys], identB[:, :], maskB[:, :].unsqueeze(1).to_broadcast([P, heads, P]),
                                  start=True, stop=False, skip_group_check=True)
                        for j in range(heads):
                            mm = pe.matmul(sc[:, j, :], qs[:, t % 3, GROUP * g + hh * heads + j, :], ks[:, b % 2, g, 0:keys],
                                           start=False, stop=(j == heads - 1), skip_group_check=True)
                        mm.then_inc(s_full[u % 2], 1)
                elif job == "peaks":
                    bk = fill((job, i))
                    pe.wait_ge(npart_done, i + 1)
                    filled(pe.transpose(bk[0:96, 0:P // 2].bitcast(BF16), npart[:, :, :].rearrange("p w h -> p (w h)"),
                                        identB[:, :]), (job, i))
                elif job == "probs":
                    t, s = divmod(i, KVH)
                    g, qt, b = ORDER[s], t % 2, t // 2
                    if s == 0:
                        pe.wait_ge(nT_done, t + 1)
                    for k in range(1 + qt):
                        u = unit(i, k)
                        if u >= 2:
                            pe.wait_ge(exp_done, u - 1)
                        else:
                            pe.wait_ge(mod_rows, 2)
                        pe.matmul(TB[u % 2][:, :], ks[:, b % 2, g, k * P:(k + 1) * P],
                                  qs[:, t % 3, GROUP * g:GROUP * (g + 1), :].rearrange("p h q -> p (h q)"),
                                  start=True, stop=False, skip_group_check=True)
                        for j in range(GROUP):
                            h = GROUP * g + j
                            mm = pe.matmul(TB[u % 2][:, j * P:(j + 1) * P], pick[:, h:h + 1].to_broadcast([96, P]), nT[:, t % 2, :],
                                           start=False, stop=(j == GROUP - 1), skip_group_check=True)
                        mm.then_inc(t_full[u % 2], 1)
                elif job == "pv":
                    t, qd = divmod(i, 2)
                    qt, b = t % 2, t // 2
                    pe.wait_ge(exp_done, unit(4 * i + 3, qt) + 1)
                    pe.wait_ge(causal, 4 * i + 4)
                    if qd == 0:
                        pe.wait_ge(v_done, t + 1)
                        if t >= 1:
                            pe.wait_ge(pv_read, t)
                    for k in range(1 + qt):
                        for c in range(4):
                            g = ORDER[4 * qd + c]
                            at = 32 * (g // 2)
                            mm = pe.matmul(OB[qd][at:at + 32, :], vone[:, b % 2, k, g, :, :].rearrange("p w d -> p (w d)"),
                                           p_turned(4 * i + c, k), start=(k == 0), stop=(k == qt), skip_group_check=True)
                    mm.then_inc(pv_done, 1)
                elif job == "wo":
                    bk = fill(("wo", i))
                    pe.wait_ge(aT_done, i + 1)
                    if i == 0:
                        pe.wait_ge(ld_wo, 16)
                    for j in range(GROUP):
                        mm = pe.matmul(bk[:, :], aT[:, j * P:(j + 1) * P], wo_sb[:, j, :], start=(j == 0), stop=(j == GROUP - 1))
                    filled(mm, ("wo", i))
                elif job == "h2T":
                    bk = fill(("h2T", i))
                    pe.wait_ge(h2_done, i + 1)
                    for k in range(KT):
                        mm = pe.transpose(bk[:, k * P:(k + 1) * P], h2[:, i % 2, k * P:(k + 1) * P], ident)
                    filled(mm, ("h2T", i))
                elif job == "route":
                    bk = fill(("gate", i))
                    pe.wait_ge(h2T_done, i + 1)
                    if i == 0:
                        pe.wait_ge(ld_gate, 64)
                    for k in range(KT):
                        mm = pe.matmul(bk[:, 0:E], h2T[:, k * P:(k + 1) * P], gate_sb[:, k, :], start=(k == 0), stop=(k == KT - 1))
                    filled(mm, ("gate", i))
                elif job == "place":
                    bk = fill(("rank", i))
                    pe.wait_ge(cnt_done, i + 1)
                    pe.matmul(bk[:, 0:E], triB[:, :], cnt[:, i, :], start=True, stop=False)
                    mm = pe.matmul(bk[:, 0:E], onesB[:, :], cum[:, i, :], start=False, stop=True)
                    filled(mm, ("rank", i))

            pe.wait_ge(rank_done, T)
            pe.wait_ge(tot_ready, 1)
            pe.matmul(OB[0][:, 0:E], onesB[:, :], cum[:, T, :], start=True, stop=True).then_inc(tot_full, 1)
            pe.wait_ge(exp_done, 3 * KVH * B)
            for i in range(TILES + 1):
                if i < TILES:
                    pe.wait_ge(ld_xe[i % 4], 16 * (i // 4 + 1))
                    if i >= 2:
                        pe.wait_ge(xT_done, i - 1)
                    for k in range(KT):
                        mm = pe.transpose(TB[i % 2][:, k * P:(k + 1) * P], xe[i % 4][:, k * P:(k + 1) * P], ident)
                    mm.then_inc(xT_full, 1)
                if i >= 1:
                    f = i - 1
                    for e in sorted({expert(f, c) for c in range(4)}):
                        r = e % RING
                        pe.wait_ge(ld_w[r], 16 * (e // RING + 1 + (r < NMOD)))
                    pe.wait_ge(xT_done, f + 1)
                    if f >= 2:
                        pe.wait_ge(y_done, f - 1)
                    if f == 0:
                        pe.wait_ge(ebp_done, 1)
                    for k in range(KT):
                        for c in range(4):
                            at = c * STRIP
                            pe.matmul(GB[f % 2][at:at + STRIP, :], xeT[:, f % 2, k * P + at:k * P + at + STRIP],
                                      ring[:, expert(f, c) % RING, k * D:(k + 1) * D], start=(k == 0), stop=False,
                                      skip_group_check=True)
                    for c in range(4):
                        e, at = expert(f, c), c * STRIP
                        mm = pe.matmul(GB[f % 2][at:at + STRIP, :], pick[:, e:e + 1].to_broadcast([96, STRIP]), ebp,
                                       start=False, stop=True, skip_group_check=True)
                    mm.then_inc(y_full, 1)
            pe.wait_ge(ctl_done, 1)
            more = pe.value_load(ctl[0:1, OVB:OVB + 1], min_val=0, max_val=OVB)
            with pe.If(more > 0):
                pe.wait_ge(y_done, TILES)
                for j in range(OVB):
                    pe.wait_ge(ov_x, 16 * (j + 1))
                    for k in range(KT):
                        mm = pe.transpose(TB[0][:, k * P:(k + 1) * P], xe[0][:, k * P:(k + 1) * P], ident)
                    mm.then_inc(ov_xT, 1)
                    pe.wait_ge(ov_w, 16 * (j + 1))
                    pe.wait_ge(ov_xTd, j + 1)
                    if j >= 1:
                        pe.wait_ge(ov_yd, j)
                    for k in range(KT):
                        pe.matmul(GB[0][:, :], xeT[:, 0, k * P:(k + 1) * P], ring[:, 0, k * D:(k + 1) * D],
                                  start=(k == 0), stop=False)
                    mm = pe.matmul(GB[0][:, :], opick[:, j:j + 1].to_broadcast([96, P]), ebp, start=False, stop=True)
                    mm.then_inc(ov_y, 1)

        @block.scalar
        def _(act):
            act.wait_ge(ld_c, 16)
            act.activation(sil[:, 0, :], cT_sb[:, :], ACT.Exp, scale=-1.0).then_inc(silu_e, 1)
            for job, i in JOBS:
                if job == "hT":
                    b = i // 2
                    bk = full(act, ("hT", i))
                    act.wait_ge(modc_done, 1)
                    if i >= 2:
                        full(act, ("kv", i - 2))
                    for k in range(KT):
                        ins = act.activation(hT[:, i % 2, k, :], bk[:, k * P:(k + 1) * P], ACT.Identity,
                                             bias=modcol[:, k, b:b + 1], scale=modcol[:, k, 32 + b:33 + b])
                    ins.then_inc(hT_done, 1)
                elif job == "split":
                    act.wait_ge(roped, i + 1)
                    if i >= 1:
                        full(act, ("stack", 5 * i - 1))
                    act.activation(qp[:, :, 2:4, :], rb[:, 0:D].rearrange("p (h o d) -> p h o d", o=1, d=HD).to_broadcast([P, H, 2, HD]),
                                   ACT.Copy)
                    act.activation(kp[:, :, 1, :], rb[:, D:D + KV].rearrange("p (h d) -> p h d", d=HD), ACT.Copy).then_inc(part1, 1)
                elif job == "rest":
                    act.wait_ge(rest1, i + 1)
                    act.activation(qp[:, :, 0:2, :], rb[:, 0:D].rearrange("p (h o d) -> p h o d", o=1, d=HD).to_broadcast([P, H, 2, HD]),
                                   ACT.Copy)
                    act.activation(kp[:, :, 2, :], rb[:, D:D + KV].rearrange("p (h d) -> p h d", d=HD), ACT.Copy).then_inc(part2, 1)
                elif job == "stack":
                    t, c = divmod(i, 5)
                    rows = full(act, (job, i))[0:96, :].bitcast(BF16)
                    if c < 4:
                        act.activation(qs[:, t % 3, 8 * c:8 * c + 8, :].rearrange("p h q -> p (h q)"), rows, ACT.Copy).then_inc(stacked, 1)
                    else:
                        act.activation(ks[:, t // 2 % 2, :, (t % 2) * P:(t % 2 + 1) * P],
                                       rows.rearrange("p (g q) -> p g q", g=KVH), ACT.Copy).then_inc(stacked, 1)
                elif job == "peaks":
                    bk = full(act, (job, i))
                    act.activation(nT[:, i % 2, :], bk[0:96, 0:P // 2].bitcast(BF16), ACT.Copy).then_inc(nT_done, 1)
                elif job == "probs":
                    for k in range(1 + i // KVH % 2):
                        u = unit(i, k)
                        act.wait_ge(t_full[u % 2], u // 2 + 1)
                        if i // 4 >= 2:
                            act.wait_ge(pv_done, i // 4 - 1)
                        act.activation(p_turned(i, k), TB[u % 2][:, :], ACT.Exp).then_inc(exp_done, 1)
                elif job == "h2T":
                    bk = full(act, ("h2T", i))
                    if i >= 1:
                        full(act, ("gate", i - 1))
                    act.activation(h2T[:, :], bk[:, :], ACT.Copy).then_inc(h2T_done, 1)
            act.wait_ge(dlt_done, 1)
            act.activation(ex[:, :], dlt[:, :], ACT.Exp).then_inc(ex_done, 1)
            for i in range(TILES + 1):
                if i < TILES:
                    act.wait_ge(xT_full, i + 1)
                    if i >= 2:
                        act.wait_ge(y_full, i - 1)
                    act.activation(xeT[:, i % 2, :], TB[i % 2][:, :], ACT.Copy).then_inc(xT_done, 1)
                if i >= 1:
                    act.wait_ge(y_done, i)
                    act.dma_start(ys[(i - 1) * P:i * P, :], ye[(i - 1) % 4]).then_inc(st_y[(i - 1) % 4], 16)
            act.wait_ge(ctl_done, 1)
            more = act.value_load(ctl[0:1, OVB:OVB + 1], min_val=0, max_val=OVB)
            with act.If(more > 0):
                for j in range(OVB):
                    act.wait_ge(ov_xT, j + 1)
                    if j >= 1:
                        act.wait_ge(ov_y, j)
                    act.activation(xeT[:, 0, :], TB[0][:, :], ACT.Copy).then_inc(ov_xTd, 1)
                    act.wait_ge(ov_yd, j + 1)
                    act.dma_start(ys[PRIM + j * CAP:PRIM + (j + 1) * CAP, :], ye[0][0:CAP, :]).then_inc(ov_st, 16)
            for t in range(T):
                act.wait_ge(gath[t % 4], 16 * TOP * (t // 4 + 1))
                act.activation(yg[t % 4][0], yg[t % 4][0], ACT.Copy, scale=cw[:, 0, t:t + 1]).then_inc(ya_done, 1)

        @block.gpsimd
        def _(pool):
            pool.memset(half[:, :], -0.5).then_inc(pool_set, 1)
            pool.memset(vone[:, :, :, :, :, :].rearrange("p b q g w d -> p (b q g w d)"), 1.0).then_inc(pool_set, 1)
            pool.memset(onesB[:, :], 1.0).then_inc(pool_set, 1)
            pool.memset(cum[:, 0, :], 0.0).then_inc(pool_set, 1)
            pool.memset(zero[:, :], 0.0).then_inc(pool_set, 1)
            pool.memset(ones[:, :], 1.0).then_inc(pool_set, 1)
            pool.wait_ge(pool_set, 6)
            for job, i in JOBS:
                if job == "ln1":
                    pool.wait_ge(stats1, i + 1)
                    pool.tensor_tensor(rstd[:, 0, i, :], veps[:, 0, i, :], half[:, 0:1], ALU.pow).then_inc(rstd1, 1)
                elif job == "bias":
                    pool.wait_ge(qk_done, 2 * (i + 1))
                    if i >= 1:
                        pool.wait_ge(roped, i)
                    pool.tensor_tensor(ra[:, :].rearrange("p (h d) -> p h d", d=HD),
                                       qk[:, :].rearrange("p (h d) -> p h d", d=HD),
                                       rope[:, i % 2, 0:1, :].to_broadcast([P, H + KVH, HD]), ALU.mult).then_inc(ropeA, 1)
                elif job == "rest":
                    pool.wait_ge(part2, i + 1)
                    pool.tensor_tensor(qp[:, :, 4, :], rb[:, 0:D].rearrange("p (h d) -> p h d", d=HD), qp[:, :, 0, :], ALU.subtract)
                    pool.tensor_tensor(kp[:, :, 0, :], rb[:, D:D + KV].rearrange("p (h d) -> p h d", d=HD), kp[:, :, 2, :],
                                       ALU.subtract).then_inc(part3, 1)
                elif job == "probs":
                    qt = i // KVH % 2
                    pool.wait_ge(exp_done, unit(i, qt) + 1)
                    place = p_turned(i, qt).rearrange("p (j q) -> p j q", j=GROUP)
                    pool.affine_select(place, place, pattern=[[0, GROUP], [1, P]], compare_op=ALU.is_ge, fill=0.0, base=0,
                                       channel_multiplier=-1).then_inc(causal, 1)
                elif job == "wo":
                    if i % 2 == 0:
                        pool.wait_ge(ld_bc[i // 2 % 2], 16 * (i // 4 + 1))
                    if i >= 1:
                        pool.wait_ge(x2_done, i)
                    pool.tensor_tensor(xg[:, :], xt[:, i, :], bc[:, i // 2 % 2, 1, :], ALU.add).then_inc(xg_done, 1)
                elif job == "ln2":
                    pool.wait_ge(stats2, i + 1)
                    pool.tensor_tensor(rstd[:, 1, i, :], veps[:, 1, i, :], half[:, 0:1], ALU.pow).then_inc(rstd2, 1)
                elif job == "pos":
                    pool.wait_ge(pos_done, i + 1)
                    if i == 0:
                        pool.wait_ge(st_zero, 16 * (TILES + OVB))
                    for s in range(TOP):
                        pool.indirect_dma_start(out=xs[0:PRIM, :], in_=h2[:, i % 2, :], in_offset=None,
                                                out_offset=bass.IndirectOffsetOnAxis(ap=posi[:, s, i:i + 1], axis=0),
                                                bounds_check=PRIM - 1, oob_is_err=False).then_inc(scat[i % 2], 16)
            pool.wait_ge(ctl_done, 1)
            more = pool.value_load(ctl[0:1, OVB:OVB + 1], min_val=0, max_val=OVB)
            with pool.If(more > 0):
                pool.wait_ge(ov_zero, 16 * OVB)
                for t in range(T):
                    pool.wait_ge(ov_h, 16 * (t + 1))
                    for s in range(TOP):
                        pool.indirect_dma_start(out=xs, in_=h2[:, 0, :], in_offset=None,
                                                out_offset=bass.IndirectOffsetOnAxis(ap=ovi[:, s, t:t + 1], axis=0),
                                                bounds_check=SLOTS - 1, oob_is_err=False).then_inc(ov_scat, 16)
                pool.wait_ge(ov_st, 16 * OVB)
            for i in range(4):
                pool.wait_ge(st_y[i], 16 * TILES // 4)
            for t in range(T):
                if t >= 4:
                    pool.wait_ge(out_done, t - 3)
                for s in range(TOP):
                    pool.indirect_dma_start(out=yg[t % 4][s], out_offset=None, in_=ys,
                                            in_offset=bass.IndirectOffsetOnAxis(ap=posgi[:, s, t:t + 1], axis=0),
                                            bounds_check=SLOTS - 1, oob_is_err=False).then_inc(gath[t % 4], 16)

        @block.vector
        def _(dve):
            taken = [0]

            def step(ins):
                taken[0] += 1
                ins.then_inc(dve_step, 1)
                dve.wait_ge(dve_step, taken[0])

            def statistics(ln, i, done):
                step(dve.bn_stats(st6[:, ln, i, :], xt[:, i, :]))
                step(dve.bn_aggr(mv[:, ln, i, :], st6[:, ln, i, :]))
                dve.tensor_scalar(veps[:, ln, i, :], mv[:, ln, i, 1:2], EPS, None, ALU.add).then_inc(done, 1)

            def gate_rows(src, rows, out_rows):
                dve.tensor_scalar(rowt[rows, 1, :], src, 0.0, 2.0, ALU.is_ge, ALU.mult)
                step(dve.tensor_scalar(rowt[rows, 0, :], src, -1.0, 0.25, ALU.mult, ALU.max))
                step(dve.tensor_tensor(rowt[rows, 0, :], rowt[rows, 0, :], src, ALU.max))
                step(dve.scalar_tensor_tensor(out=out_rows, in0=rowt[rows, 1, :], scalar=-1.0, in1=rowt[rows, 0, :],
                                              op0=ALU.add, op1=ALU.mult))

            dve.wait_ge(silu_e, 1)
            step(dve.tensor_scalar(sil[:, 1, :], sil[:, 0, :], 1.0, None, ALU.add))
            step(dve.reciprocal(sil[:, 0, :], sil[:, 1, :]))
            rows = [v.rearrange("p (k b) -> p k b", b=B).unsqueeze(2).to_broadcast([P, KT, 8, B]) for v in (sil[:, 0, :], cT_sb[:, :])]
            dve.tensor_tensor(sil8[:, :, :, :], rows[0], rows[1], ALU.mult).then_inc(silu_done, 1)
            dve.wait_ge(ld_const, 16)
            dve.tensor_copy(identB[:, :], cst[:, C_ID:C_ID + P])
            dve.tensor_copy(maskB[:, :], cst[:, C_MASK:C_MASK + P])
            for w in range(3):
                dve.tensor_copy(pick[32 * w:32 * (w + 1), :], cst[32 * w:32 * (w + 1), C_ID + 32 * w:C_ID + 32 * (w + 1)])
            dve.tensor_copy(triB[:, :], cst[:, C_TRI:C_TRI + P]).then_inc(cast_done, 1)

            for job, i in JOBS:
                if job == "mods" and i == 0:
                    dve.wait_ge(mod_mm, 1)
                    dve.tensor_copy(modA[0:32, :], TB[0][0:32, :])
                    dve.tensor_scalar(modA[32:64, :], TB[0][32:64, :], 1.0, None, ALU.add).then_inc(mod_rows, 1)
                    bk = full(dve, ("mcol", 0))
                    dve.tensor_copy(modcol[:, :, :], bk[:, 0:KT * 64].rearrange("p (k m) -> p k m", k=KT)).then_inc(modc_done, 1)
                elif job == "mods":
                    dve.wait_ge(mod_mm, 2)
                    dve.wait_ge(ld_bias, 32)
                    gate_rows(TB[0][64:96, :], slice(64, 96), modA[64:96, :])
                    dve.tensor_tensor(rowt[64:96, 0, :], modA[64:96, :], bo_bc[64:96, :], ALU.mult)
                    dve.tensor_copy(modA[96:128, :], TB[0][96:128, :])
                    dve.tensor_scalar(modB[0:32, :], TB[1][0:32, :], 1.0, None, ALU.add)
                    gate_rows(TB[1][32:64, :], slice(32, 64), modB[32:64, :])
                    dve.tensor_copy(ejf[:, 0:1], cst[:, 0:1]).then_inc(mod_rows, 1)
                elif job == "ln1":
                    dve.wait_ge(ld_x[min(i, 1)] if i < 2 else ld_x[0], 16 if i < 2 else 32)
                    statistics(0, i, stats1)
                elif job == "xh":
                    dve.wait_ge(rstd1, i + 1)
                    if i >= 2:
                        full(dve, ("hT", i - 2))
                    dve.tensor_scalar(xh[:, i % 2, :], xt[:, i, :], mv[:, 0, i, 0:1], rstd[:, 0, i, :],
                                      ALU.subtract, ALU.mult).then_inc(xh_done, 1)
                elif job == "bias":
                    b, qt = i // 2, i % 2
                    bk = full(dve, ("q", i))
                    if i == 0:
                        dve.wait_ge(ld_bias, 32)
                        dve.wait_ge(pool_set, 6)
                    dve.tensor_tensor(qk[:, 0:D], bk[:, :], bqkv_bc[:, 0:D], ALU.add).then_inc(qk_done, 1)
                    bk = full(dve, ("kv", i))
                    dve.tensor_tensor(qk[:, D:D + KV], bk[:, 0:KV], bqkv_bc[:, D:D + KV], ALU.add).then_inc(qk_done, 1)
                    if i >= 4:
                        dve.wait_ge(pv_done, 2 * (i - 2))
                    dve.tensor_tensor(vone[:, b % 2, qt, :, 0, :], bk[:, KV:2 * KV].rearrange("p (g d) -> p g d", d=HD),
                                      bqkv_bc[:, D + KV:QKV].rearrange("p (g d) -> p g d", d=HD), ALU.add).then_inc(v_done, 1)
                elif job == "rope":
                    qt = i % 2
                    dve.wait_ge(qk_done, 2 * (i + 1))
                    if i >= 1:
                        dve.wait_ge(part3, i)
                    pairs = qk[:, :].rearrange("p (h d two) -> p h d two", h=H + KVH, two=2)
                    sin = rope[:, qt, 1:2, :].rearrange("p o (d two) -> p o d two", two=2)
                    turned = rb[:, :].rearrange("p (h d two) -> p h d two", h=H + KVH, two=2)
                    for w in range(2):
                        ins = dve.tensor_tensor(turned[:, :, :, w], pairs[:, :, :, 1 - w],
                                                sin[:, :, :, w].to_broadcast([P, H + KVH, HD // 2]), ALU.mult)
                    step(ins)
                    dve.wait_ge(ropeA, i + 1)
                    dve.tensor_tensor(rb[:, :], rb[:, :], ra[:, :], ALU.add).then_inc(roped, 1)
                elif job == "split":
                    dve.wait_ge(roped, i + 1)
                    dve.wait_ge(part1, i + 1)
                    rq = rb[:, 0:D].rearrange("p (h d) -> p h d", d=HD)
                    rk = rb[:, D:D + KV].rearrange("p (h d) -> p h d", d=HD)
                    dve.tensor_tensor(rq, rq, qp[:, :, 2, :], ALU.subtract)
                    dve.tensor_tensor(rk, rk, kp[:, :, 1, :], ALU.subtract).then_inc(rest1, 1)
                elif job == "peak":
                    t, s = divmod(i, KVH)
                    g, qt = ORDER[s], t % 2
                    heads, keys = GROUP // (1 + qt), P * (1 + qt)
                    for hh in range(1 + qt):
                        u = unit(i, hh)
                        dve.wait_ge(s_full[u % 2], u // 2 + 1)
                        dve.tensor_reduce(nmax[:, t % 2, g, hh * heads:(hh + 1) * heads],
                                          SB[u % 2][:, :].rearrange("p (h k) -> p h k", k=keys), AX.X, ALU.max,
                                          negate=True).then_inc(max_done, 1)
                elif job == "parts":
                    dve.wait_ge(max_done, unit(KVH * i + KVH - 1, i % 2) + 1)
                    if i >= 1:
                        full(dve, ("peaks", i - 1))
                    left = nmax[:, i % 2, :, :].rearrange("p g j -> p (g j)")
                    for w in range(2):
                        step(dve.tensor_copy(npart[:, w, :], left))
                        step(dve.tensor_tensor(nrem[:, w, :], left, npart[:, w, :], ALU.subtract))
                        left = nrem[:, w, :]
                    dve.tensor_copy(npart[:, 2, :], left).then_inc(npart_done, 1)
                elif job == "sums":
                    dve.wait_ge(pv_done, 2 * (i + 1))
                    if i >= 1:
                        dve.wait_ge(x2_done, i)
                    for w in range(2):
                        ins = dve.transpose(pvT[:, w, :, :, :].rearrange("p b v d -> p (b v d)"), OB[w][:, :])
                    ins.then_inc(pv_read, 1)
                    dve.wait_ge(pv_read, i + 1)
                    step(dve.reciprocal(zinv[:, :, :], pvT[:, :, :, 1, 0]))
                elif job == "norm":
                    for w in range(2):
                        ins = dve.tensor_tensor(pvT[:, 0, :, w, :], pvT[:, w, :, 0, :], zinv[:, w, :].unsqueeze(2).to_broadcast([P, 16, HD]), ALU.mult)
                    step(ins)
                    if i >= 1:
                        full(dve, ("wo", i - 1))
                    dve.transpose(aT[:, :], pvT[:, 0, :, :, :].rearrange("p b w d -> p (b w d)")).then_inc(aT_done, 1)
                elif job == "x2":
                    if i % 2 == 0:
                        dve.wait_ge(ld_bc[i // 2 % 2], 16 * (i // 4 + 1))
                    bk = full(dve, ("wo", i))
                    dve.tensor_tensor(t2, bk[:, :], bc[:, i // 2 % 2, 0, :], ALU.mult).then_inc(att_done, 1)
                    dve.wait_ge(att_done, i + 1)
                    dve.wait_ge(xg_done, i + 1)
                    dve.tensor_tensor(xt[:, i, :], t2, xg[:, :], ALU.add).then_inc(x2_done, 1)
                elif job == "ln2":
                    dve.wait_ge(x2_done, i + 1)
                    statistics(1, i, stats2)
                    step(dve.scalar_tensor_tensor(out=hm[:, :], in0=xt[:, i, :], scalar=mv[:, 1, i, 0:1],
                                                  in1=bc[:, i // 2 % 2, 2, :], op0=ALU.subtract, op1=ALU.mult))
                elif job == "h2":
                    dve.wait_ge(rstd2, i + 1)
                    if i >= 2:
                        dve.wait_ge(scat[i % 2], 16 * TOP * (i // 2))
                        dve.wait_ge(st_h[i % 2], 16 * (i // 2))
                        full(dve, ("h2T", i - 2))
                    dve.scalar_tensor_tensor(out=h2[:, i % 2, :], in0=hm[:, :], scalar=rstd[:, 1, i, :],
                                             in1=bc[:, i // 2 % 2, 3, :], op0=ALU.mult, op1=ALU.add).then_inc(h2_done, 1)
                    if i == T - 1:
                        full(dve, ("kv", T - 1))
                        dve.wait_ge(ld_gate, 64)
                        second, third = slice(E, 2 * E), slice(2 * E, 3 * E)
                        step(dve.tensor_copy(ebp, eb_sb[:, :]))
                        step(dve.tensor_tensor(eb_sb[:, :], eb_sb[:, :], ebp, ALU.subtract))
                        step(dve.tensor_copy(ebp[second, :], eb_sb[second, :]))
                        step(dve.tensor_copy(ebp[third, :], eb_sb[third, :]))
                        step(dve.tensor_tensor(eb_sb[third, :], eb_sb[third, :], ebp[third, :], ALU.subtract))
                        dve.tensor_copy(ebp[third, :], eb_sb[third, :]).then_inc(ebp_done, 1)
                elif job == "choose":
                    bk = full(dve, ("gate", i))
                    dve.tensor_copy(lg[:, :], bk[:, 0:E]).then_inc(lg_done, 1)
                    dve.wait_ge(lg_done, i + 1)
                    step(dve.max(top[:, i, :], lg[:, :]))
                    step(dve.max_index(tid[:, :], top[:, i, :], lg[:, :]))
                    step(dve.tensor_copy(tif[:, :], tid[:, :]))
                    for s in range(TOP):
                        ins = dve.tensor_scalar(oh[:, s, i, :], iota, tif[:, s:s + 1], None, ALU.is_equal)
                    step(ins)
                    dve.tensor_tensor(cnt[:, i, :], oh[:, 0, i, :], oh[:, 1, i, :], ALU.add).then_inc(cnt_done, 1)
                    dve.wait_ge(cnt_done, i + 1)
                    ins = dve.tensor_tensor(cum[:, i + 1, :], cum[:, i, :], cnt[:, i, :], ALU.add)
                    if i == T - 1:
                        ins.then_inc(tot_ready, 1)
                    else:
                        step(ins)
                elif job == "pos":
                    bk = full(dve, ("rank", i))
                    dve.tensor_scalar(pa[:, 0, :], bk[:, 0:E], float(CAP), BIG, ALU.is_ge, ALU.mult)
                    dve.tensor_tensor(pa[:, 1, :], bk[:, 0:E], base, ALU.add).then_inc(rank_done, 1)
                    dve.wait_ge(rank_done, i + 1)
                    step(dve.tensor_tensor(pa[:, 0, :], pa[:, 0, :], pa[:, 1, :], ALU.add))
                    step(dve.tensor_tensor(pp[:, :, :], oh[:, :, i, :], pa[:, 0:1, :].to_broadcast([P, TOP, E]), ALU.mult))
                    step(dve.tensor_reduce(pos[:, :, i], pp[:, :, :], AX.X, ALU.add))
                    dve.tensor_copy(posi[:, :, i], pos[:, :, i]).then_inc(pos_done, 1)

            dve.tensor_tensor(dlt[:, :], top[:, :, 1], top[:, :, 0], ALU.subtract).then_inc(dlt_done, 1)
            dve.wait_ge(ex_done, 1)
            step(dve.tensor_scalar(e1[:, :], ex[:, :], 1.0, None, ALU.add))
            step(dve.reciprocal(cw[:, 0, :], e1[:, :]))
            step(dve.tensor_tensor(cw[:, 1, :], ex[:, :], cw[:, 0, :], ALU.mult))
            dve.wait_ge(tot_full, 1)
            step(dve.tensor_tensor(nbm[:, :, :], OB[0][:, 0:E].unsqueeze(2).to_broadcast([P, E, MOST]),
                                   cst[:, C_THR:C_THR + MOST].unsqueeze(1).to_broadcast([P, E, MOST]), ALU.is_gt))
            step(dve.tensor_reduce(nb[:, :], nbm[:, :, :], AX.X, ALU.add))
            step(dve.tensor_tensor_scan(inc[:, :], ones[:, :], nb[:, :], 0.0, ALU.mult, ALU.add))
            step(dve.tensor_tensor(de[:, 0, :], inc[:, :], nb[:, :], ALU.subtract))
            step(dve.tensor_scalar(de[:, 1, :], de[:, 0, :], float(CAP), PRIM - CAP - BIG, ALU.mult, ALU.add))
            step(dve.tensor_tensor(de[:, 2, :], de[:, 1, :], base, ALU.subtract))
            for s in range(TOP):
                ins = dve.tensor_tensor(ohd[:, s, :, :], oh[:, s, :, :], de[:, 2:3, :].to_broadcast([P, T, E]), ALU.mult)
            step(ins)
            dve.tensor_scalar(far[:, :, :], pos[:, :, :], BIG, None, ALU.is_ge)
            step(dve.tensor_reduce(dsel[:, :, :], ohd[:, :, :, :], AX.X, ALU.add))
            step(dve.tensor_tensor(dsel[:, :, :], dsel[:, :, :], far[:, :, :], ALU.mult))
            dve.tensor_scalar(ovf[:, :, :], far[:, :, :], -BIG, BIG, ALU.mult, ALU.add)
            step(dve.tensor_tensor(posg[:, :, :], pos[:, :, :], dsel[:, :, :], ALU.add))
            step(dve.tensor_tensor(ovf[:, :, :], ovf[:, :, :], posg[:, :, :], ALU.add))
            dve.tensor_copy(posgi[:, :, :], posg[:, :, :])
            dve.tensor_copy(ovi[:, :, :], ovf[:, :, :])
            step(dve.tensor_tensor(ejm[:, :, :], inc[:, :].unsqueeze(1).to_broadcast([P, OVB + 1, E]),
                                   cst[:, C_J:C_J + OVB + 1].unsqueeze(2).to_broadcast([P, OVB + 1, E]), ALU.is_le))
            step(dve.tensor_reduce(ejf[:, :], ejm[:, :, :], AX.X, ALU.add))
            step(dve.tensor_copy(ejf[:, OVB:OVB + 1], inc[:, E - 1:E]))
            dve.tensor_scalar(opick[:, :], ejf[0:96, 0:OVB], cst[0:96, C_MOD:C_MOD + 1], None, ALU.is_equal)
            dve.tensor_scalar(ctl[:, :], ejf[:, :], float(E - 1), None, ALU.min).then_inc(ctl_done, 1)

            for i in range(TILES):
                dve.wait_ge(y_full, i + 1)
                if i >= 4:
                    dve.wait_ge(st_y[i % 4], 16 * (i // 4))
                dve.tensor_copy(ye[i % 4], GB[i % 2][:, :]).then_inc(y_done, 1)
            more = dve.value_load(ctl[0:1, OVB:OVB + 1], min_val=0, max_val=OVB)
            with dve.If(more > 0):
                for i in range(4):
                    dve.wait_ge(st_y[i], 16 * TILES // 4)
                for j in range(OVB):
                    dve.wait_ge(ov_y, j + 1)
                    if j >= 1:
                        dve.wait_ge(ov_st, 16 * j)
                    dve.tensor_copy(ye[0], GB[0][:, :]).then_inc(ov_yd, 1)
            dve.wait_ge(ld_gb, 16)
            for t in range(T):
                ya, yb = yg[t % 4]
                dve.wait_ge(gath[t % 4], 16 * TOP * (t // 4 + 1))
                dve.wait_ge(ya_done, t + 1)
                step(dve.scalar_tensor_tensor(out=yb, in0=yb, scalar=cw[:, 1, t:t + 1], in1=ya, op0=ALU.mult, op1=ALU.add))
                step(dve.tensor_tensor(yb, yb, bc[:, 0, t // 2, :], ALU.mult))
                dve.tensor_tensor(xt[:, t, :], xt[:, t, :], yb, ALU.add).then_inc(out_done, 1)


def constants():
    import numpy as np
    c = np.zeros((P, C_END), np.float32)
    r = np.arange(P)
    c[:, C_ID:C_ID + P] = np.eye(P)
    c[:, C_MASK:C_MASK + P] = np.where(r[None, :] <= r[:, None], 0.0, -1e20)
    c[:, C_TRI:C_TRI + P] = r[:, None] < r[None, :]
    c[:, C_IOTA:C_IOTA + E] = np.arange(E)
    c[:, C_BASE:C_BASE + E] = np.arange(E) * CAP
    c[:, C_THR:C_THR + MOST] = np.arange(1, MOST + 1) * CAP
    c[:, C_J:C_J + OVB + 1] = np.arange(OVB + 1)
    c[:, C_MOD] = r % E
    inv = (1.0 / np.float32(10000.0) ** (np.arange(0, HD, 2, dtype=np.float32) / np.float32(HD))).astype(np.float32)
    angle = np.arange(S, dtype=np.float32)[:, None] * inv[None, :]
    cos, sin = 0.5 * np.cos(angle), 0.5 * np.sin(angle)
    table = np.stack([np.stack([cos, cos], -1).reshape(S, HD), np.stack([-sin, sin], -1).reshape(S, HD)], 1)
    c[:, C_ROPE:C_END] = table.reshape(QTS, P, 2, HD).transpose(1, 0, 2, 3).reshape(P, -1)
    return c


def kernel(**inputs):
    import numpy as np
    import concourse.bacc as bacc
    from concourse.bass_utils import run_bass_kernel_spmd

    a = {k: np.asarray(v) for k, v in inputs.items()}
    arrays = {
        "x": a["L0_attn_x"].reshape(B * S, D),
        "cT": a["L0_c"].T.reshape(KT, P, B).transpose(1, 0, 2).reshape(P, KT * B),
        "wmod": a["L0_wmod"].reshape(KT, P, NMOD, D).transpose(2, 1, 0, 3).reshape(NMOD, P, KT * D),
        "wqkv": a["L0_attn_w_qkv"].T.reshape(KT, P, QKV).transpose(1, 0, 2),
        "bqkv": a["L0_attn_b_qkv"],
        "wo": a["L0_attn_w_o"].T.reshape(KVH, GROUP, HD, D).transpose(0, 2, 1, 3).reshape(P, GROUP, D),
        "bo": a["L0_attn_b_o"],
        "gate": a["L0_ffn_gate_w"].T.reshape(KT, P, E).transpose(1, 0, 2),
        "ew": a["L0_ffn_expert_w"].transpose(0, 2, 1).reshape(E, KT, P, D).transpose(0, 2, 1, 3).reshape(E, P, KT * D),
        "eb": a["L0_ffn_expert_b"],
        "const": constants(),
    }
    arrays = {f"in_{k}": np.ascontiguousarray(v) for k, v in arrays.items()}
    nc = bacc.Bacc("TRN2", target_bir_lowering=False, num_devices=1)
    args = [nc.dram_tensor(k, v.shape, mybir.dt.from_np(v.dtype), kind="ExternalInput").ap() for k, v in arrays.items()]
    out = nc.dram_tensor("out", (B * S, D), F32, kind="ExternalOutput").ap()
    program(nc, *args, out)
    r = run_bass_kernel_spmd(nc, [arrays], core_ids=[0])
    return r.results[0]["out"].reshape(B, S, D)
```

```python
import concourse.bass as bass
from concourse import mybir
from contextlib import ExitStack

F32 = mybir.dt.float32
BF16 = mybir.dt.bfloat16
I32 = mybir.dt.int32
U32 = mybir.dt.uint32
ALU = mybir.AluOpType
ACT = mybir.ActivationFunctionType
AX = mybir.AxisListType

B, S, D = 4, 256, 512
H, KVH, HD = 32, 8, 16
GROUP = H // KVH
E, TOP = 32, 2
P = 128
KT = D // P
QTS = S // P
T = B * QTS
KV = KVH * HD
QKV = D + 2 * KV
EPS = 1e-5
NMOD = 6

ORDER = [0, 2, 4, 6, 1, 3, 5, 7]
STEPS = T * KVH
PAIRS = 6

CAP = 96
PRIM = E * CAP
STRIP = 32
TILES = PRIM // P
OVB = (B * S * TOP - 1) // CAP
MOST = (B * S - 1) // CAP
SLOTS = PRIM + OVB * CAP
BIG = 65536.0
RING = 8
TURN = RING * CAP // P
TURNS = TILES // TURN
YBUF = 3
KEPT = 4

C_ID, C_MASK, C_TRI, C_IOTA, C_BASE, C_THR = 0, P, 2 * P, 3 * P, 3 * P + E, 3 * P + 2 * E
C_J = C_THR + MOST
C_MOD = C_J + OVB + 1
C_ROPE = C_MOD + 1
C_END = C_ROPE + QTS * 2 * HD


def unit(n, h):
    t, i = divmod(n, KVH)
    return (t // 2) * 3 * KVH + (i if t % 2 == 0 else KVH + 2 * i + h)


def expert(i, c):
    return (i * P + c * STRIP) // CAP


def ended(i):
    return [e for e in range(E) if ((e + 1) * CAP - 1) // P == i]


WHEN = {"ln1": -20.0, "xh": -18.7, "hT": -16.0, "qkv": -15.5, "bias": -15.4, "rope": -14.9, "split": -12.9,
        "rest": -11.8, "parts": -1.8, "peaks": -0.9, "sums": 10.5, "norm": 12.7, "wo": 14.2, "x2": 14.7,
        "ln2": 15.2, "h2": 16.9, "h2T": 19.0, "route": 19.4, "choose": 21.1, "place": 24.2, "pos": 24.4}
STACKS = (-10.7, -10.69, -10.68, -9.9, -9.29)
LEAD = 8.9
LAG = 1.3
MODS = (-18, -12.5)
EARLY = 6.0


def schedule():
    jobs = [(at, "mods", i) for i, at in enumerate(MODS)]
    for t in range(T):
        for name, at in WHEN.items():
            early = EARLY if t == 1 and at < WHEN["rope"] else 0
            jobs.append((KVH * t + at - early, name, t))
        jobs += [(KVH * t + at, "stack", 5 * t + c) for c, at in enumerate(STACKS)]
    jobs += [(n, "probs", n) for n in range(STEPS)]
    jobs += [(n - LEAD, "peak", n) for n in range(STEPS)]
    jobs += [(4 * i + 3 + LAG, "pv", i) for i in range(STEPS // 4)]
    return [(name, i) for _, name, i in sorted(jobs)]


def bank_uses(jobs):
    uses, n = {}, 0
    fills = {"hT": ["hT"], "qkv": ["q", "kv"], "stack": ["stack"], "peaks": ["peaks"], "wo": ["wo"], "h2T": ["h2T"],
             "route": ["gate"], "place": ["rank"]}
    for job, i in jobs:
        for name in ["mcol"] if (job, i) == ("mods", 0) else fills.get(job, []):
            uses[(name, i)] = n
            n += 1
    return uses


def program(nc, x, cT, wmod, wqkv, bqkv, wo, bo, gate, ew, eb, const, out):
    JOBS = schedule()
    USES = bank_uses(JOBS)

    ctx = ExitStack()
    with ctx:
        def sb(name, shape, dt=F32):
            return ctx.enter_context(nc.sbuf_tensor(name, shape, dt))

        def sem(name):
            return ctx.enter_context(nc.semaphore(name))

        modrow = nc.dram_tensor("modrow", (5, B, D), F32, kind="Internal").ap()
        xs = nc.dram_tensor("xs", (SLOTS, D), F32, kind="Internal").ap()
        ys = nc.dram_tensor("ys", (SLOTS, D), F32, kind="Internal").ap()
        hs = nc.dram_tensor("hs", (T * P, D), F32, kind="Internal").ap()

        ring = sb("ring", [P, RING, KT * D])
        xt = sb("xt", [P, T, D])
        wqkv_sb = sb("wqkv_sb", [P, KT, QKV])
        wo_sb = sb("wo_sb", [P, GROUP, D])
        gate_sb = sb("gate_sb", [P, KT, E])
        bqkv_bc = sb("bqkv_bc", [P, QKV])
        eb_sb = sb("eb_sb", [3 * E, D])
        cst = sb("cst", [P, C_END])
        identB = sb("identB", [P, P], BF16)
        maskB = sb("maskB", [P, P], BF16)
        triB = sb("triB", [P, P], BF16)
        onesB = sb("onesB", [P, P], BF16)
        cT_sb = sb("cT_sb", [P, KT * B])
        sil = sb("sil", [P, 2, KT * B])
        modcol = sb("modcol", [P, KT, 64])
        bc = sb("bc", [P, 2, 4, D])
        st6 = sb("st6", [P, 2, T, 6])
        mv = sb("mv", [P, 2, T, 2])
        veps = sb("veps", [P, 2, T, 1])
        rstd = sb("rstd", [P, 2, T, 1])
        half = sb("half", [P, 1])
        xh = sb("xh", [P, 2, D])
        hT = sb("hT", [P, 2, KT, P])
        qk = sb("qk", [P, D + KV])
        ra = sb("ra", [P, D + KV])
        rb = sb("rb", [P, D + KV])
        qp = sb("qp", [P, H, PAIRS, HD], BF16)
        kp = sb("kp", [P, KVH, PAIRS, HD], BF16)
        qs = sb("qs", [96, 3, H, P], BF16)
        ks = sb("ks", [96, 2, KVH, S], BF16)
        vone = sb("vone", [P, 2, QTS, KVH, 2, HD])
        nmax = sb("nmax", [P, 2, KVH, GROUP])
        nrem = sb("nrem", [P, 2, H])
        npart = sb("npart", [P, 3, H], BF16)
        nT = sb("nT", [96, 2, P], BF16)
        pick = sb("pick", [96, H], BF16)
        turn_pick = sb("turn_pick", [96, RING], BF16)
        opick = sb("opick", [96, OVB], BF16)
        pvT = sb("pvT", [P, 2, 16, 2, HD])
        zinv = sb("zinv", [P, 2, 16])
        aT = sb("aT", [P, GROUP * P])
        xg = sb("xg", [P, D])
        t2 = pvT[:, 1, :, :, :].rearrange("p b w d -> p (b w d)")
        h2 = sb("h2", [P, 2, D])
        hm = sb("hm", [P, D])
        h2T = sb("h2T", [P, KT * P])
        lg = sb("lg", [P, E])
        top = sb("top", [P, T, 8])
        tid = sb("tid", [P, 8], U32)
        tif = sb("tif", [P, 8])
        cw = sb("cw", [P, TOP, T])
        oh = sb("oh", [P, TOP, T, E])
        cnt = sb("cnt", [P, T, E], BF16)
        cum = sb("cum", [P, T + 1, E], BF16)
        pa = sb("pa", [P, 2, E])
        pp = sb("pp", [P, TOP, E])
        pos = sb("pos", [P, TOP, T])
        posi = sb("posi", [P, TOP, T], I32)
        posg = sb("posg", [P, TOP, T])
        posgi = sb("posgi", [P, TOP, T], I32)
        ovi = sb("ovi", [P, TOP, T], I32)
        ones = sb("ones", [P, E])
        ctl = sb("ctl", [P, OVB + 1], I32)
        zero = sb("zero", [P, D // 8])

        sil8 = aT[:, 0:KT * 8 * B].rearrange("p (k r b) -> p k r b", r=8, b=B)
        modA, modB, rowt, bo_bc = hm, h2T, h2, xg
        spare = wqkv_sb[:, :, :].rearrange("p k n -> p (k n)")
        ohd = spare[:, 0:TOP * T * E].rearrange("p (s t e) -> p s t e", s=TOP, t=T)
        nbm = spare[:, 512:832].rearrange("p (e m) -> p e m", e=E)
        ejm = spare[:, 832:1536].rearrange("p (j e) -> p j e", e=E)
        nb = spare[:, 1536:1568]
        inc = spare[:, 1568:1600]
        de = spare[:, 1600:1696].rearrange("p (s e) -> p s e", e=E)
        far, dsel, ovf = (spare[:, at:at + TOP * T].rearrange("p (s t) -> p s t", t=T) for at in (1696, 1712, 1728))
        ejf = spare[:, 1744:1744 + OVB + 1]
        dlt, ex, e1 = (spare[:, at:at + T] for at in (1768, 1776, 1784))
        ebp = spare[0:3 * E, 1792:2048].bitcast(BF16)
        xe = [xh[:, 0, :], xh[:, 1, :], ra[:, 0:D], rb[:, 0:D], qk[:, 0:D], hm[:, :]]
        xeT = hT[:, :, :, :].rearrange("p s k q -> p s (k q)")
        ye = [bc[:, 1, i, :] for i in range(YBUF)]
        yg = [[xg[:, :], aT[:, :]], [h2T[:, :], hm[:, :]], [ra[:, 0:D], rb[:, 0:D]], [qk[:, 0:D], t2]]

        def bank(name):
            return ctx.enter_context(nc.psum_tensor(name, [P, 512], F32))
        SB = [bank(f"SB{i}") for i in range(2)]
        TB = [bank(f"TB{i}") for i in range(2)]
        OB = [bank(f"OB{i}") for i in range(2)]
        GB = [bank(f"GB{i}") for i in range(2)]

        ld_x = [sem(f"ld_x{i}") for i in range(2)]
        ld_c = sem("ld_c")
        ld_const = sem("ld_const")
        ld_wqkv = sem("ld_wqkv")
        ld_bias = sem("ld_bias")
        ld_wo = sem("ld_wo")
        ld_gate = sem("ld_gate")
        ld_w = [sem(f"ld_w{i}") for i in range(RING)]
        ld_bc = [sem(f"ld_bc{i}") for i in range(2)]
        ld_gb = sem("ld_gb")
        st_mod = sem("st_mod")
        st_zero = sem("st_zero")
        st_h = [sem(f"st_h{i}") for i in range(2)]
        pool_set = sem("pool_set")
        dve_step = sem("dve_step")
        cast_done = sem("cast_done")
        silu_e = sem("silu_e")
        silu_done = sem("silu_done")
        mod_mm = sem("mod_mm")
        mod_rows = sem("mod_rows")
        modc_done = sem("modc_done")
        g_full = [sem(f"g_full{i}") for i in range(2)]
        stats1 = sem("stats1")
        stats2 = sem("stats2")
        rstd1 = sem("rstd1")
        rstd2 = sem("rstd2")
        xh_done = sem("xh_done")
        hT_done = sem("hT_done")
        qk_done = sem("qk_done")
        v_done = sem("v_done")
        ropeA = sem("ropeA")
        roped = sem("roped")
        part1 = sem("part1")
        rest1 = sem("rest1")
        part2 = sem("part2")
        part3 = sem("part3")
        stacked = sem("stacked")
        s_full = [sem(f"s_full{i}") for i in range(2)]
        max_done = sem("max_done")
        npart_done = sem("npart_done")
        nT_done = sem("nT_done")
        t_full = [sem(f"t_full{i}") for i in range(2)]
        exp_done = sem("exp_done")
        pv_done = sem("pv_done")
        pv_read = sem("pv_read")
        aT_done = sem("aT_done")
        xg_done = sem("xg_done")
        att_done = sem("att_done")
        x2_done = sem("x2_done")
        h2_done = sem("h2_done")
        h2T_done = sem("h2T_done")
        lg_done = sem("lg_done")
        cnt_done = sem("cnt_done")
        rank_done = sem("rank_done")
        pos_done = sem("pos_done")
        scat = [sem(f"scat{i}") for i in range(2)]
        tot_ready = sem("tot_ready")
        tot_full = sem("tot_full")
        dlt_done = sem("dlt_done")
        ex_done = sem("ex_done")
        ctl_done = sem("ctl_done")
        ebp_done = sem("ebp_done")
        picks = sem("picks")
        ya_done = sem("ya_done")
        ld_xe = [sem(f"ld_xe{i}") for i in range(TURN)]
        xT_full = sem("xT_full")
        xT_done = sem("xT_done")
        y_full = sem("y_full")
        y_done = sem("y_done")
        st_y = [sem(f"st_y{i}") for i in range(YBUF)]
        ov_zero = sem("ov_zero")
        ov_h = sem("ov_h")
        ov_scat = sem("ov_scat")
        gath = [sem(f"gath{i}") for i in range(4)]
        out_done = sem("out_done")
        st_out = sem("st_out")

        ident = cst[:, C_ID:C_ID + P]
        iota = cst[:, C_IOTA:C_IOTA + E]
        base = cst[:, C_BASE:C_BASE + E]
        rope = cst[:, C_ROPE:C_END].rearrange("p (q s d) -> p q s d", q=QTS, s=2)

        def full(eng, key):
            n = USES[key]
            eng.wait_ge(g_full[n % 2], n // 2 + 1)
            return GB[n % 2]

        def read_signal(key):
            name, i = key
            return {"mcol": (modc_done, 1), "hT": (hT_done, i + 1), "q": (qk_done, 2 * i + 1), "kv": (v_done, i + 1),
                    "stack": (stacked, i + 1), "peaks": (nT_done, i + 1),
                    "wo": (att_done, i + 1), "h2T": (h2T_done, i + 1), "gate": (lg_done, i + 1),
                    "rank": (rank_done, i + 1)}[name]

        KEYS = {n: key for key, n in USES.items()}

        def p_turned(n, k):
            c = n % 4
            at = (2 * (c % 2) + k) * 512
            return ring[:, KEPT + 2 * (n // 4 % 2) + c // 2, at:at + 512]

        block = ctx.enter_context(nc.Block())

        @block.sync
        def _(sp):
            def load_mod(m):
                sp.dma_start(ring[:, m, :], wmod[m]).then_inc(ld_w[m], 16)

            sp.dma_start(cT_sb[:, :], cT).then_inc(ld_c, 16)
            for m in range(2):
                load_mod(m)
            sp.dma_start(xt[:, 0, :], x[0:P, :]).then_inc(ld_x[0], 16)
            sp.dma_start(cst[:, :], const).then_inc(ld_const, 16)
            sp.dma_start(xt[:, 1, :], x[P:2 * P, :]).then_inc(ld_x[1], 16)
            sp.dma_start(wqkv_sb[:, :, :], wqkv).then_inc(ld_wqkv, 16)
            sp.dma_start(bqkv_bc[:, :], bqkv.partition_broadcast(P)).then_inc(ld_bias, 16)
            sp.dma_start(bo_bc[:, :], bo.partition_broadcast(P)).then_inc(ld_bias, 16)
            for m in range(2, NMOD):
                load_mod(m)
            sp.wait_ge(ld_x[0], 16)
            sp.dma_start(xt[:, 2:T, :], x[2 * P:, :].rearrange("(t p) d -> p t d", p=P)).then_inc(ld_x[0], 16)
            sp.dma_start(wo_sb[:, :, :], wo).then_inc(ld_wo, 16)
            sp.dma_start(gate_sb[:, :, :], gate).then_inc(ld_gate, 16)
            for w in range(3):
                sp.dma_start(eb_sb[32 * w:32 * (w + 1), :], eb).then_inc(ld_gate, 16)
            sp.wait_ge(mod_rows, 2)
            sp.dma_start(modrow[0], modA[64:64 + B, :]).then_inc(st_mod, 16)
            sp.dma_start(modrow[1], rowt[64:64 + B, 0, :]).then_inc(st_mod, 16)
            sp.dma_start(modrow[2], modB[0:B, :]).then_inc(st_mod, 16)
            sp.dma_start(modrow[3], modA[96:96 + B, :]).then_inc(st_mod, 16)
            sp.dma_start(modrow[4], modB[32:32 + B, :]).then_inc(st_mod, 16)
            sp.wait_ge(st_mod, 80)
            for b in range(2):
                sp.dma_start(bc[:, b, :, :], modrow[0:4, b, :].partition_broadcast(P)).then_inc(ld_bc[b], 16)
            sp.wait_ge(mod_mm, 2)
            for e in range(KEPT):
                sp.dma_start(ring[:, e, :], ew[e]).then_inc(ld_w[e], 16)
            sp.sem_inc(xT_done, 2)
            sp.sem_inc(y_done, 2)
            sp.wait_ge(pool_set, 5)
            def nothing(rows):
                return zero[0:rows, :].unsqueeze(1).to_broadcast([rows, 8, D // 8])

            with sp.Fori(0, TILES) as i:
                sp.dma_start(xs[bass.ds(i * P, P), :].rearrange("p (w d) -> p w d", w=8), nothing(P)).then_inc(st_zero, 16)
            with sp.Fori(0, OVB) as j:
                sp.dma_start(ys[bass.ds(j * CAP + PRIM, CAP), :].rearrange("p (w d) -> p w d", w=8), nothing(CAP)).then_inc(st_zero, 16)
            for t in range(T):
                sp.wait_ge(h2_done, t + 1)
                sp.dma_start(hs[t * P:(t + 1) * P, :], h2[:, t % 2, :]).then_inc(st_h[t % 2], 16)
                if t % 2 == 1 and t < T - 1:
                    b = t // 2 + 2
                    if b < B:
                        sp.dma_start(bc[:, b % 2, :, :], modrow[0:4, b, :].partition_broadcast(P)).then_inc(ld_bc[b % 2], 16)
                    elif b == B:
                        sp.dma_start(bc[:, 0, :, :], modrow[4].partition_broadcast(P)).then_inc(ld_gb, 16)
                if t == T - 2:
                    sp.wait_ge(pv_done, STEPS // 4)
                    for e in range(KEPT, RING):
                        sp.dma_start(ring[:, e, :], ew[e]).then_inc(ld_w[e], 16)
            for i in range(2):
                sp.wait_ge(scat[i], 16 * TOP * T // 2)
            for u in range(TURN):
                sp.dma_start(xe[u], xs[u * P:(u + 1) * P, :]).then_inc(ld_xe[u], 16)
            with sp.Fori(0, TURNS - 1) as n:
                for u in range(TURN):
                    sp.wait_ge(xT_full, n * TURN + (u + 1))
                    sp.dma_start(xe[u], xs[bass.ds(n * (TURN * P) + (TURN + u) * P, P), :]).then_inc(ld_xe[u], 16)
                    for e in ended(u):
                        sp.wait_ge(y_full, n * TURN + (u + 1))
                        sp.dma_start(ring[:, e:e + 1, :], ew[bass.ds(n * RING + (RING + e), 1), :, :].rearrange("e p n -> p e n")).then_inc(ld_w[e], 16)
            sp.wait_ge(ctl_done, 1)
            more = sp.value_load(ctl[0:1, OVB:OVB + 1], min_val=0, max_val=OVB)
            with sp.If(more > 0):
                with sp.Fori(0, OVB) as j:
                    sp.dma_start(xs[bass.ds(j * CAP + PRIM, CAP), :].rearrange("p (w d) -> p w d", w=8), nothing(CAP)).then_inc(ov_zero, 16)
                for i in range(2):
                    sp.wait_ge(st_h[i], 16 * T // 2)
                for t in range(T):
                    if t >= 1:
                        sp.wait_ge(ov_scat, 16 * TOP * t)
                    sp.dma_start(h2[:, 0, :], hs[t * P:(t + 1) * P, :]).then_inc(ov_h, 16)
                sp.wait_ge(ov_scat, 16 * TOP * T)
                with sp.Fori(0, OVB) as j:
                    sp.wait_ge(y_full, j + TILES)
                    of = sp.value_load(ctl[0:1, bass.ds(j, 1)], min_val=0, max_val=E - 1)
                    sp.dma_start(ring[:, 0:1, :], ew[bass.ds(of, 1), :, :].rearrange("e p n -> p e n")).then_inc(ld_w[0], 16)
                    sp.dma_start(xe[0][0:CAP, :], xs[bass.ds(j * CAP + PRIM, CAP), :]).then_inc(ld_xe[0], 16)
            for t in range(T):
                sp.wait_ge(out_done, t + 1)
                sp.dma_start(out[t * P:(t + 1) * P, :], xt[:, t, :]).then_inc(st_out, 16)
            sp.wait_ge(st_out, 16 * T)
            for i in range(2):
                sp.wait_ge(st_h[i], 16 * T // 2)

        @block.tensor
        def _(pe):
            def fill(key):
                n = USES[key]
                if n >= 2:
                    signal, count = read_signal(KEYS[n - 2])
                    pe.wait_ge(signal, count)
                return GB[n % 2]

            def filled(ins, key):
                ins.then_inc(g_full[USES[key] % 2], 1)

            def modulation(ms):
                for m in ms:
                    pe.wait_ge(ld_w[m], 16)
                for k in range(KT):
                    for m in ms:
                        at = 32 * (m % 4)
                        mm = pe.matmul(TB[m // 4][at:at + 32, :],
                                       sil8[:, k, :, :].rearrange("p r b -> p (r b)"),
                                       ring[:, m, k * D:(k + 1) * D], start=(k == 0), stop=(k == KT - 1))
                mm.then_inc(mod_mm, 1)

            for job, i in JOBS:
                if job == "mods" and i == 0:
                    pe.wait_ge(silu_done, 1)
                    modulation([0, 1])
                    bk = fill(("mcol", 0))
                    pe.wait_ge(ld_const, 16)
                    pe.wait_ge(cast_done, 1)
                    pe.wait_ge(mod_rows, 1)
                    for k in range(KT):
                        mm = pe.transpose(bk[:, k * 64:(k + 1) * 64], modA[0:64, k * P:(k + 1) * P], cst[0:64, C_ID:C_ID + 64])
                    filled(mm, ("mcol", 0))
                elif job == "mods":
                    modulation(range(2, NMOD))
                elif job == "hT":
                    bk = fill(("hT", i))
                    pe.wait_ge(xh_done, i + 1)
                    for k in range(KT):
                        mm = pe.transpose(bk[:, k * P:(k + 1) * P], xh[:, i % 2, k * P:(k + 1) * P], ident)
                    filled(mm, ("hT", i))
                elif job == "qkv":
                    bk = fill(("q", i))
                    pe.wait_ge(hT_done, i + 1)
                    if i == 0:
                        pe.wait_ge(ld_wqkv, 16)
                    for k in range(KT):
                        mm = pe.matmul(bk[:, :], hT[:, i % 2, k, :], wqkv_sb[:, k, 0:D], start=(k == 0), stop=(k == KT - 1))
                    filled(mm, ("q", i))
                    bk = fill(("kv", i))
                    for k in range(KT):
                        mm = pe.matmul(bk[:, 0:2 * KV], hT[:, i % 2, k, :], wqkv_sb[:, k, D:QKV],
                                       start=(k == 0), stop=(k == KT - 1))
                    filled(mm, ("kv", i))
                elif job == "stack":
                    t, c = divmod(i, 5)
                    pe.wait_ge(part1, t + 1)
                    pe.wait_ge(part2, t + 1)
                    pe.wait_ge(part3, t + 1)
                    rows = fill((job, i))[:, :].bitcast(BF16)
                    for u in range(8):
                        src = qp[:, 8 * c + u, :, :] if c < 4 else kp[:, u, :, :]
                        mm = pe.transpose(rows[0:96, u * P:(u + 1) * P], src.rearrange("p w d -> p (w d)"), identB[:, :])
                    filled(mm, (job, i))
                elif job == "peak":
                    t, s = divmod(i, KVH)
                    g, qt, b = ORDER[s], t % 2, t // 2
                    if s == 0:
                        pe.wait_ge(stacked, 5 * (t + 1))
                    heads, keys = GROUP // (1 + qt), P * (1 + qt)
                    for hh in range(1 + qt):
                        u = unit(i, hh)
                        if u >= 2:
                            pe.wait_ge(max_done, u - 1)
                        sc = SB[u % 2][:, :].rearrange("p (h k) -> p h k", k=keys)
                        pe.matmul(sc[:, :, keys - P:keys], identB[:, :], maskB[:, :].unsqueeze(1).to_broadcast([P, heads, P]),
                                  start=True, stop=False, skip_group_check=True)
                        for j in range(heads):
                            mm = pe.matmul(sc[:, j, :], qs[:, t % 3, GROUP * g + hh * heads + j, :], ks[:, b % 2, g, 0:keys],
                                           start=False, stop=(j == heads - 1), skip_group_check=True)
                        mm.then_inc(s_full[u % 2], 1)
                elif job == "peaks":
                    bk = fill((job, i))
                    pe.wait_ge(npart_done, i + 1)
                    filled(pe.transpose(bk[0:96, 0:P // 2].bitcast(BF16), npart[:, :, :].rearrange("p w h -> p (w h)"),
                                        identB[:, :]), (job, i))
                elif job == "probs":
                    t, s = divmod(i, KVH)
                    g, qt, b = ORDER[s], t % 2, t // 2
                    if s == 0:
                        pe.wait_ge(nT_done, t + 1)
                    for k in range(1 + qt):
                        u = unit(i, k)
                        if u >= 2:
                            pe.wait_ge(exp_done, u - 1)
                        else:
                            pe.wait_ge(mod_rows, 2)
                        pe.matmul(TB[u % 2][:, :], ks[:, b % 2, g, k * P:(k + 1) * P],
                                  qs[:, t % 3, GROUP * g:GROUP * (g + 1), :].rearrange("p h q -> p (h q)"),
                                  start=True, stop=False, skip_group_check=True)
                        if k == qt:
                            pe.matmul(TB[u % 2][:, :].rearrange("p (j q) -> p j q", j=GROUP), maskB[:, :],
                                      identB[:, :].unsqueeze(1).to_broadcast([P, GROUP, P]), start=False, stop=False,
                                      skip_group_check=True)
                        for j in range(GROUP):
                            h = GROUP * g + j
                            mm = pe.matmul(TB[u % 2][:, j * P:(j + 1) * P], pick[:, h:h + 1].to_broadcast([96, P]), nT[:, t % 2, :],
                                           start=False, stop=(j == GROUP - 1), skip_group_check=True)
                        mm.then_inc(t_full[u % 2], 1)
                elif job == "pv":
                    t, qd = divmod(i, 2)
                    qt, b = t % 2, t // 2
                    pe.wait_ge(exp_done, unit(4 * i + 3, qt) + 1)
                    if qd == 0:
                        pe.wait_ge(v_done, t + 1)
                        if t >= 1:
                            pe.wait_ge(pv_read, t)
                    for k in range(1 + qt):
                        for c in range(4):
                            g = ORDER[4 * qd + c]
                            at = 32 * (g // 2)
                            mm = pe.matmul(OB[qd][at:at + 32, :], vone[:, b % 2, k, g, :, :].rearrange("p w d -> p (w d)"),
                                           p_turned(4 * i + c, k), start=(k == 0), stop=(k == qt), skip_group_check=True)
                    mm.then_inc(pv_done, 1)
                elif job == "wo":
                    bk = fill(("wo", i))
                    pe.wait_ge(aT_done, i + 1)
                    if i == 0:
                        pe.wait_ge(ld_wo, 16)
                    for j in range(GROUP):
                        mm = pe.matmul(bk[:, :], aT[:, j * P:(j + 1) * P], wo_sb[:, j, :], start=(j == 0), stop=(j == GROUP - 1))
                    filled(mm, ("wo", i))
                elif job == "h2T":
                    bk = fill(("h2T", i))
                    pe.wait_ge(h2_done, i + 1)
                    for k in range(KT):
                        mm = pe.transpose(bk[:, k * P:(k + 1) * P], h2[:, i % 2, k * P:(k + 1) * P], ident)
                    filled(mm, ("h2T", i))
                elif job == "route":
                    bk = fill(("gate", i))
                    pe.wait_ge(h2T_done, i + 1)
                    if i == 0:
                        pe.wait_ge(ld_gate, 64)
                    for k in range(KT):
                        mm = pe.matmul(bk[:, 0:E], h2T[:, k * P:(k + 1) * P], gate_sb[:, k, :], start=(k == 0), stop=(k == KT - 1))
                    filled(mm, ("gate", i))
                elif job == "place":
                    bk = fill(("rank", i))
                    pe.wait_ge(cnt_done, i + 1)
                    pe.matmul(bk[:, 0:E], triB[:, :], cnt[:, i, :], start=True, stop=False)
                    mm = pe.matmul(bk[:, 0:E], onesB[:, :], cum[:, i, :], start=False, stop=True)
                    filled(mm, ("rank", i))

            pe.wait_ge(rank_done, T)
            pe.wait_ge(tot_ready, 1)
            pe.matmul(OB[0][:, 0:E], onesB[:, :], cum[:, T, :], start=True, stop=True).then_inc(tot_full, 1)
            pe.wait_ge(exp_done, 3 * KVH * B)
            def turn_rows(n, u):
                pe.wait_ge(ld_xe[u % TURN], (n + u // TURN) * 16 + 16)
                pe.wait_ge(xT_done, n * TURN + (u + 1))
                for k in range(KT):
                    mm = pe.transpose(TB[u % 2][:, k * P:(k + 1) * P], xe[u % TURN][:, k * P:(k + 1) * P], ident)
                mm.then_inc(xT_full, 1)

            def multiply(n, u):
                for r in sorted({expert(u, c) for c in range(4)}):
                    pe.wait_ge(ld_w[r], n * 16 + 16 * (1 + (r < NMOD)))
                pe.wait_ge(xT_done, n * TURN + (u + 3))
                pe.wait_ge(y_done, n * TURN + (u + 1))
                for k in range(KT):
                    for c in range(4):
                        at = c * STRIP
                        pe.matmul(GB[u % 2][at:at + STRIP, :], xeT[:, u % 2, k * P + at:k * P + at + STRIP],
                                  ring[:, expert(u, c), k * D:(k + 1) * D], start=(k == 0), stop=False, skip_group_check=True)
                if u == 0:
                    pe.wait_ge(picks, n + 1)
                for c in range(4):
                    at, e = c * STRIP, expert(u, c)
                    mm = pe.matmul(GB[u % 2][at:at + STRIP, :], turn_pick[:, e:e + 1].to_broadcast([96, STRIP]), ebp,
                                   start=False, stop=True, skip_group_check=True)
                mm.then_inc(y_full, 1)

            pe.wait_ge(ebp_done, 1)
            turn_rows(0, 0)
            with pe.Fori(0, TURNS - 1) as n:
                for u in range(TURN):
                    turn_rows(n, u + 1)
                    multiply(n, u)
            for u in range(TURN):
                if u + 1 < TURN:
                    turn_rows(TURNS - 1, u + 1)
                multiply(TURNS - 1, u)
            pe.wait_ge(ctl_done, 1)
            more = pe.value_load(ctl[0:1, OVB:OVB + 1], min_val=0, max_val=OVB)
            with pe.If(more > 0):
                with pe.Fori(0, OVB) as j:
                    pe.wait_ge(ld_xe[0], j * 16 + 16 * (TURNS + 1))
                    pe.wait_ge(xT_done, j + (TILES + 2))
                    for k in range(KT):
                        mm = pe.transpose(TB[0][:, k * P:(k + 1) * P], xe[0][:, k * P:(k + 1) * P], ident)
                    mm.then_inc(xT_full, 1)
                    pe.wait_ge(ld_w[0], j * 16 + 16 * (TURNS + 2))
                    pe.wait_ge(xT_done, j + (TILES + 3))
                    pe.wait_ge(y_done, j + (TILES + 2))
                    for k in range(KT):
                        pe.matmul(GB[0][:, :], xeT[:, 0, k * P:(k + 1) * P], ring[:, 0, k * D:(k + 1) * D],
                                  start=(k == 0), stop=False)
                    pe.matmul(GB[0][:, :], opick[:, bass.ds(j, 1)].to_broadcast([96, P]), ebp, start=False, stop=True).then_inc(y_full, 1)

        @block.scalar
        def _(act):
            act.wait_ge(ld_c, 16)
            act.activation(sil[:, 0, :], cT_sb[:, :], ACT.Exp, scale=-1.0).then_inc(silu_e, 1)
            for job, i in JOBS:
                if job == "hT":
                    b = i // 2
                    bk = full(act, ("hT", i))
                    act.wait_ge(modc_done, 1)
                    if i >= 2:
                        full(act, ("kv", i - 2))
                    for k in range(KT):
                        ins = act.activation(hT[:, i % 2, k, :], bk[:, k * P:(k + 1) * P], ACT.Identity,
                                             bias=modcol[:, k, b:b + 1], scale=modcol[:, k, 32 + b:33 + b])
                    ins.then_inc(hT_done, 1)
                elif job == "split":
                    act.wait_ge(roped, i + 1)
                    if i >= 1:
                        full(act, ("stack", 5 * i - 1))
                    rq = rb[:, 0:D].rearrange("p (h o d) -> p h o d", o=1, d=HD)
                    rk = rb[:, D:D + KV].rearrange("p (h o d) -> p h o d", o=1, d=HD)
                    act.activation(qp[:, :, 0:3, :], rq.to_broadcast([P, H, 3, HD]), ACT.Copy)
                    act.activation(kp[:, :, 0:4:3, :], rk.to_broadcast([P, KVH, 2, HD]), ACT.Copy)
                    act.activation(kp[:, :, 5:6, :], rk, ACT.Copy).then_inc(part1, 1)
                elif job == "rest":
                    act.wait_ge(rest1, i + 1)
                    rq = rb[:, 0:D].rearrange("p (h o d) -> p h o d", o=1, d=HD)
                    rk = rb[:, D:D + KV].rearrange("p (h o d) -> p h o d", o=1, d=HD)
                    act.activation(qp[:, :, 3:5, :], rq.to_broadcast([P, H, 2, HD]), ACT.Copy)
                    act.activation(kp[:, :, 1:5:3, :], rk.to_broadcast([P, KVH, 2, HD]), ACT.Copy).then_inc(part2, 1)
                elif job == "stack":
                    t, c = divmod(i, 5)
                    rows = full(act, (job, i))[0:96, :].bitcast(BF16)
                    if c < 4:
                        act.activation(qs[:, t % 3, 8 * c:8 * c + 8, :].rearrange("p h q -> p (h q)"), rows, ACT.Copy).then_inc(stacked, 1)
                    else:
                        act.activation(ks[:, t // 2 % 2, :, (t % 2) * P:(t % 2 + 1) * P],
                                       rows.rearrange("p (g q) -> p g q", g=KVH), ACT.Copy).then_inc(stacked, 1)
                elif job == "peaks":
                    bk = full(act, (job, i))
                    act.activation(nT[:, i % 2, :], bk[0:96, 0:P // 2].bitcast(BF16), ACT.Copy).then_inc(nT_done, 1)
                elif job == "probs":
                    for k in range(1 + i // KVH % 2):
                        u = unit(i, k)
                        act.wait_ge(t_full[u % 2], u // 2 + 1)
                        if i // 4 >= 2:
                            act.wait_ge(pv_done, i // 4 - 1)
                        act.activation(p_turned(i, k), TB[u % 2][:, :], ACT.Exp).then_inc(exp_done, 1)
                elif job == "h2T":
                    bk = full(act, ("h2T", i))
                    if i >= 1:
                        full(act, ("gate", i - 1))
                    act.activation(h2T[:, :], bk[:, :], ACT.Copy).then_inc(h2T_done, 1)
            act.wait_ge(dlt_done, 1)
            act.activation(ex[:, :], dlt[:, :], ACT.Exp).then_inc(ex_done, 1)
            def columns(n, u):
                act.wait_ge(xT_full, n * TURN + (u + 1))
                if not (isinstance(n, int) and n * TURN + u < 2):
                    act.wait_ge(y_full, n * TURN + (u - 1))
                act.activation(xeT[:, u % 2, :], TB[u % 2][:, :], ACT.Copy).then_inc(xT_done, 1)

            def store(n, u):
                act.wait_ge(y_done, n * TURN + (u + 3))
                act.dma_start(ys[bass.ds(n * (TURN * P) + u * P, P), :], ye[u % YBUF]).then_inc(st_y[u % YBUF], 16)

            columns(0, 0)
            columns(0, 1)
            with act.Fori(0, TURNS - 1) as n:
                for u in range(TURN):
                    store(n, u)
                    columns(n, u + 2)
            for u in range(TURN):
                store(TURNS - 1, u)
                if u + 2 < TURN:
                    columns(TURNS - 1, u + 2)
            act.wait_ge(ctl_done, 1)
            more = act.value_load(ctl[0:1, OVB:OVB + 1], min_val=0, max_val=OVB)
            with act.If(more > 0):
                with act.Fori(0, OVB) as j:
                    act.wait_ge(xT_full, j + (TILES + 1))
                    act.wait_ge(y_full, j + TILES)
                    act.activation(xeT[:, 0, :], TB[0][:, :], ACT.Copy).then_inc(xT_done, 1)
                    act.wait_ge(y_done, j + (TILES + 3))
                    act.dma_start(ys[bass.ds(j * CAP + PRIM, CAP), :], ye[0][0:CAP, :]).then_inc(st_y[0], 16)
            for t in range(T):
                act.wait_ge(gath[t % 4], 16 * TOP * (t // 4 + 1))
                act.activation(yg[t % 4][0], yg[t % 4][0], ACT.Copy, scale=cw[:, 0, t:t + 1]).then_inc(ya_done, 1)

        @block.gpsimd
        def _(pool):
            pool.memset(half[:, :], -0.5).then_inc(pool_set, 1)
            pool.memset(vone[:, :, :, :, :, :].rearrange("p b q g w d -> p (b q g w d)"), 1.0).then_inc(pool_set, 1)
            pool.memset(onesB[:, :], 1.0).then_inc(pool_set, 1)
            pool.memset(cum[:, 0, :], 0.0).then_inc(pool_set, 1)
            pool.memset(zero[:, :], 0.0).then_inc(pool_set, 1)
            pool.memset(ones[:, :], 1.0).then_inc(pool_set, 1)
            pool.wait_ge(pool_set, 6)
            for job, i in JOBS:
                if job == "ln1":
                    pool.wait_ge(stats1, i + 1)
                    pool.tensor_tensor(rstd[:, 0, i, :], veps[:, 0, i, :], half[:, 0:1], ALU.pow).then_inc(rstd1, 1)
                elif job == "bias":
                    pool.wait_ge(qk_done, 2 * (i + 1))
                    if i >= 1:
                        pool.wait_ge(roped, i)
                    pool.tensor_tensor(ra[:, :].rearrange("p (h d) -> p h d", d=HD),
                                       qk[:, :].rearrange("p (h d) -> p h d", d=HD),
                                       rope[:, i % 2, 0:1, :].to_broadcast([P, H + KVH, HD]), ALU.mult).then_inc(ropeA, 1)
                elif job == "rest":
                    pool.wait_ge(part2, i + 1)
                    pool.tensor_tensor(qp[:, :, 5, :], rb[:, 0:D].rearrange("p (h d) -> p h d", d=HD), qp[:, :, 3, :], ALU.subtract)
                    pool.tensor_tensor(kp[:, :, 2, :], rb[:, D:D + KV].rearrange("p (h d) -> p h d", d=HD), kp[:, :, 1, :],
                                       ALU.subtract).then_inc(part3, 1)
                elif job == "wo":
                    if i % 2 == 0:
                        pool.wait_ge(ld_bc[i // 2 % 2], 16 * (i // 4 + 1))
                    if i >= 1:
                        pool.wait_ge(x2_done, i)
                    pool.tensor_tensor(xg[:, :], xt[:, i, :], bc[:, i // 2 % 2, 1, :], ALU.add).then_inc(xg_done, 1)
                elif job == "ln2":
                    pool.wait_ge(stats2, i + 1)
                    pool.tensor_tensor(rstd[:, 1, i, :], veps[:, 1, i, :], half[:, 0:1], ALU.pow).then_inc(rstd2, 1)
                elif job == "pos":
                    pool.wait_ge(pos_done, i + 1)
                    if i == 0:
                        pool.wait_ge(st_zero, 16 * (TILES + OVB))
                    for s in range(TOP):
                        pool.indirect_dma_start(out=xs[0:PRIM, :], in_=h2[:, i % 2, :], in_offset=None,
                                                out_offset=bass.IndirectOffsetOnAxis(ap=posi[:, s, i:i + 1], axis=0),
                                                bounds_check=PRIM - 1, oob_is_err=False).then_inc(scat[i % 2], 16)
            pool.tensor_copy(turn_pick[:, :], pick[:, 0:RING]).then_inc(picks, 1)
            with pool.Fori(1, TURNS) as n:
                pool.wait_ge(y_full, n * TURN)
                pool.tensor_copy(turn_pick[:, :], pick[:, bass.ds(n * RING, RING)]).then_inc(picks, 1)
            pool.wait_ge(ctl_done, 1)
            more = pool.value_load(ctl[0:1, OVB:OVB + 1], min_val=0, max_val=OVB)
            with pool.If(more > 0):
                pool.wait_ge(ov_zero, 16 * OVB)
                for t in range(T):
                    pool.wait_ge(ov_h, 16 * (t + 1))
                    for s in range(TOP):
                        pool.indirect_dma_start(out=xs, in_=h2[:, 0, :], in_offset=None,
                                                out_offset=bass.IndirectOffsetOnAxis(ap=ovi[:, s, t:t + 1], axis=0),
                                                bounds_check=SLOTS - 1, oob_is_err=False).then_inc(ov_scat, 16)
                pool.wait_ge(st_y[0], 16 * (TILES // YBUF + OVB))
            for i in range(YBUF):
                pool.wait_ge(st_y[i], 16 * TILES // YBUF)
            for t in range(T):
                if t >= 4:
                    pool.wait_ge(out_done, t - 3)
                for s in range(TOP):
                    pool.indirect_dma_start(out=yg[t % 4][s], out_offset=None, in_=ys,
                                            in_offset=bass.IndirectOffsetOnAxis(ap=posgi[:, s, t:t + 1], axis=0),
                                            bounds_check=SLOTS - 1, oob_is_err=False).then_inc(gath[t % 4], 16)

        @block.vector
        def _(dve):
            taken = [0]

            def step(ins):
                taken[0] += 1
                ins.then_inc(dve_step, 1)
                dve.wait_ge(dve_step, taken[0])

            def statistics(ln, i, done):
                step(dve.bn_stats(st6[:, ln, i, :], xt[:, i, :]))
                step(dve.bn_aggr(mv[:, ln, i, :], st6[:, ln, i, :]))
                dve.tensor_scalar(veps[:, ln, i, :], mv[:, ln, i, 1:2], EPS, None, ALU.add).then_inc(done, 1)

            def gate_rows(src, rows, out_rows):
                dve.tensor_scalar(rowt[rows, 1, :], src, 0.0, 2.0, ALU.is_ge, ALU.mult)
                step(dve.tensor_scalar(rowt[rows, 0, :], src, -1.0, 0.25, ALU.mult, ALU.max))
                step(dve.tensor_tensor(rowt[rows, 0, :], rowt[rows, 0, :], src, ALU.max))
                return dve.scalar_tensor_tensor(out=out_rows, in0=rowt[rows, 1, :], scalar=-1.0, in1=rowt[rows, 0, :],
                                                op0=ALU.add, op1=ALU.mult)

            dve.wait_ge(silu_e, 1)
            step(dve.tensor_scalar(sil[:, 1, :], sil[:, 0, :], 1.0, None, ALU.add))
            step(dve.reciprocal(sil[:, 0, :], sil[:, 1, :]))
            rows = [v.rearrange("p (k b) -> p k b", b=B).unsqueeze(2).to_broadcast([P, KT, 8, B]) for v in (sil[:, 0, :], cT_sb[:, :])]
            dve.tensor_tensor(sil8[:, :, :, :], rows[0], rows[1], ALU.mult).then_inc(silu_done, 1)
            dve.wait_ge(ld_const, 16)
            dve.tensor_copy(identB[:, :], cst[:, C_ID:C_ID + P])
            dve.tensor_copy(maskB[:, :], cst[:, C_MASK:C_MASK + P])
            for w in range(3):
                dve.tensor_copy(pick[32 * w:32 * (w + 1), :], cst[32 * w:32 * (w + 1), C_ID + 32 * w:C_ID + 32 * (w + 1)])
            dve.tensor_copy(triB[:, :], cst[:, C_TRI:C_TRI + P]).then_inc(cast_done, 1)

            for job, i in JOBS:
                if job == "mods" and i == 0:
                    dve.wait_ge(mod_mm, 1)
                    dve.tensor_copy(modA[0:32, :], TB[0][0:32, :])
                    dve.tensor_scalar(modA[32:64, :], TB[0][32:64, :], 1.0, None, ALU.add).then_inc(mod_rows, 1)
                    bk = full(dve, ("mcol", 0))
                    dve.tensor_copy(modcol[:, :, :], bk[:, 0:KT * 64].rearrange("p (k m) -> p k m", k=KT)).then_inc(modc_done, 1)
                elif job == "mods":
                    dve.wait_ge(mod_mm, 2)
                    dve.wait_ge(ld_bias, 32)
                    step(gate_rows(TB[0][64:96, :], slice(64, 96), modA[64:96, :]))
                    dve.tensor_tensor(rowt[64:96, 0, :], modA[64:96, :], bo_bc[64:96, :], ALU.mult)
                    dve.tensor_copy(modA[96:128, :], TB[0][96:128, :])
                    dve.tensor_scalar(modB[0:32, :], TB[1][0:32, :], 1.0, None, ALU.add)
                    gate_rows(TB[1][32:64, :], slice(32, 64), modB[32:64, :]).then_inc(mod_rows, 1)
                elif job == "ln1":
                    dve.wait_ge(ld_x[min(i, 1)] if i < 2 else ld_x[0], 16 if i < 2 else 32)
                    statistics(0, i, stats1)
                elif job == "xh":
                    dve.wait_ge(rstd1, i + 1)
                    if i >= 2:
                        full(dve, ("hT", i - 2))
                    dve.tensor_scalar(xh[:, i % 2, :], xt[:, i, :], mv[:, 0, i, 0:1], rstd[:, 0, i, :],
                                      ALU.subtract, ALU.mult).then_inc(xh_done, 1)
                elif job == "bias":
                    b, qt = i // 2, i % 2
                    bk = full(dve, ("q", i))
                    if i == 0:
                        dve.wait_ge(ld_bias, 32)
                        dve.wait_ge(pool_set, 6)
                    dve.tensor_tensor(qk[:, 0:D], bk[:, :], bqkv_bc[:, 0:D], ALU.add).then_inc(qk_done, 1)
                    bk = full(dve, ("kv", i))
                    dve.tensor_tensor(qk[:, D:D + KV], bk[:, 0:KV], bqkv_bc[:, D:D + KV], ALU.add).then_inc(qk_done, 1)
                    if i >= 4:
                        dve.wait_ge(pv_done, 2 * (i - 2))
                    dve.tensor_tensor(vone[:, b % 2, qt, :, 0, :], bk[:, KV:2 * KV].rearrange("p (g d) -> p g d", d=HD),
                                      bqkv_bc[:, D + KV:QKV].rearrange("p (g d) -> p g d", d=HD), ALU.add).then_inc(v_done, 1)
                elif job == "rope":
                    qt = i % 2
                    dve.wait_ge(qk_done, 2 * (i + 1))
                    if i >= 1:
                        dve.wait_ge(part3, i)
                    pairs = qk[:, :].rearrange("p (h d two) -> p h d two", h=H + KVH, two=2)
                    sin = rope[:, qt, 1:2, :].rearrange("p o (d two) -> p o d two", two=2)
                    turned = rb[:, :].rearrange("p (h d two) -> p h d two", h=H + KVH, two=2)
                    for w in range(2):
                        ins = dve.tensor_tensor(turned[:, :, :, w], pairs[:, :, :, 1 - w],
                                                sin[:, :, :, w].to_broadcast([P, H + KVH, HD // 2]), ALU.mult)
                    step(ins)
                    dve.wait_ge(ropeA, i + 1)
                    dve.tensor_tensor(rb[:, :], rb[:, :], ra[:, :], ALU.add).then_inc(roped, 1)
                elif job == "split":
                    dve.wait_ge(roped, i + 1)
                    dve.wait_ge(part1, i + 1)
                    rq = rb[:, 0:D].rearrange("p (h d) -> p h d", d=HD)
                    rk = rb[:, D:D + KV].rearrange("p (h d) -> p h d", d=HD)
                    dve.tensor_tensor(rq, rq, qp[:, :, 0, :], ALU.subtract)
                    dve.tensor_tensor(rk, rk, kp[:, :, 0, :], ALU.subtract).then_inc(rest1, 1)
                elif job == "peak":
                    t, s = divmod(i, KVH)
                    g, qt = ORDER[s], t % 2
                    heads, keys = GROUP // (1 + qt), P * (1 + qt)
                    for hh in range(1 + qt):
                        u = unit(i, hh)
                        dve.wait_ge(s_full[u % 2], u // 2 + 1)
                        dve.tensor_reduce(nmax[:, t % 2, g, hh * heads:(hh + 1) * heads],
                                          SB[u % 2][:, :].rearrange("p (h k) -> p h k", k=keys), AX.X, ALU.max,
                                          negate=True).then_inc(max_done, 1)
                elif job == "parts":
                    dve.wait_ge(max_done, unit(KVH * i + KVH - 1, i % 2) + 1)
                    if i >= 1:
                        full(dve, ("peaks", i - 1))
                    left = nmax[:, i % 2, :, :].rearrange("p g j -> p (g j)")
                    for w in range(2):
                        step(dve.tensor_copy(npart[:, w, :], left))
                        step(dve.tensor_tensor(nrem[:, w, :], left, npart[:, w, :], ALU.subtract))
                        left = nrem[:, w, :]
                    dve.tensor_copy(npart[:, 2, :], left).then_inc(npart_done, 1)
                elif job == "sums":
                    dve.wait_ge(pv_done, 2 * (i + 1))
                    if i >= 1:
                        dve.wait_ge(x2_done, i)
                    for w in range(2):
                        ins = dve.transpose(pvT[:, w, :, :, :].rearrange("p b v d -> p (b v d)"), OB[w][:, :])
                    ins.then_inc(pv_read, 1)
                    dve.wait_ge(pv_read, i + 1)
                    step(dve.reciprocal(zinv[:, :, :], pvT[:, :, :, 1, 0]))
                elif job == "norm":
                    for w in range(2):
                        ins = dve.tensor_tensor(pvT[:, 0, :, w, :], pvT[:, w, :, 0, :], zinv[:, w, :].unsqueeze(2).to_broadcast([P, 16, HD]), ALU.mult)
                    step(ins)
                    if i >= 1:
                        full(dve, ("wo", i - 1))
                    dve.transpose(aT[:, :], pvT[:, 0, :, :, :].rearrange("p b w d -> p (b w d)")).then_inc(aT_done, 1)
                elif job == "x2":
                    if i % 2 == 0:
                        dve.wait_ge(ld_bc[i // 2 % 2], 16 * (i // 4 + 1))
                    bk = full(dve, ("wo", i))
                    dve.tensor_tensor(t2, bk[:, :], bc[:, i // 2 % 2, 0, :], ALU.mult).then_inc(att_done, 1)
                    dve.wait_ge(att_done, i + 1)
                    dve.wait_ge(xg_done, i + 1)
                    dve.tensor_tensor(xt[:, i, :], t2, xg[:, :], ALU.add).then_inc(x2_done, 1)
                elif job == "ln2":
                    dve.wait_ge(x2_done, i + 1)
                    statistics(1, i, stats2)
                    step(dve.scalar_tensor_tensor(out=hm[:, :], in0=xt[:, i, :], scalar=mv[:, 1, i, 0:1],
                                                  in1=bc[:, i // 2 % 2, 2, :], op0=ALU.subtract, op1=ALU.mult))
                elif job == "h2":
                    dve.wait_ge(rstd2, i + 1)
                    if i >= 2:
                        dve.wait_ge(scat[i % 2], 16 * TOP * (i // 2))
                        dve.wait_ge(st_h[i % 2], 16 * (i // 2))
                        full(dve, ("h2T", i - 2))
                    dve.scalar_tensor_tensor(out=h2[:, i % 2, :], in0=hm[:, :], scalar=rstd[:, 1, i, :],
                                             in1=bc[:, i // 2 % 2, 3, :], op0=ALU.mult, op1=ALU.add).then_inc(h2_done, 1)
                    if i == T - 1:
                        full(dve, ("kv", T - 1))
                        dve.wait_ge(ld_gate, 64)
                        second, third = slice(E, 2 * E), slice(2 * E, 3 * E)
                        step(dve.tensor_copy(ebp, eb_sb[:, :]))
                        step(dve.tensor_tensor(eb_sb[:, :], eb_sb[:, :], ebp, ALU.subtract))
                        step(dve.tensor_copy(ebp[second, :], eb_sb[second, :]))
                        step(dve.tensor_copy(ebp[third, :], eb_sb[third, :]))
                        step(dve.tensor_tensor(eb_sb[third, :], eb_sb[third, :], ebp[third, :], ALU.subtract))
                        dve.tensor_copy(ebp[third, :], eb_sb[third, :]).then_inc(ebp_done, 1)
                elif job == "choose":
                    bk = full(dve, ("gate", i))
                    dve.tensor_copy(lg[:, :], bk[:, 0:E]).then_inc(lg_done, 1)
                    dve.wait_ge(lg_done, i + 1)
                    step(dve.max(top[:, i, :], lg[:, :]))
                    step(dve.max_index(tid[:, :], top[:, i, :], lg[:, :]))
                    step(dve.tensor_copy(tif[:, :], tid[:, :]))
                    for s in range(TOP):
                        ins = dve.tensor_scalar(oh[:, s, i, :], iota, tif[:, s:s + 1], None, ALU.is_equal)
                    step(ins)
                    dve.tensor_tensor(cnt[:, i, :], oh[:, 0, i, :], oh[:, 1, i, :], ALU.add).then_inc(cnt_done, 1)
                    dve.wait_ge(cnt_done, i + 1)
                    ins = dve.tensor_tensor(cum[:, i + 1, :], cum[:, i, :], cnt[:, i, :], ALU.add)
                    if i == T - 1:
                        ins.then_inc(tot_ready, 1)
                    else:
                        step(ins)
                elif job == "pos":
                    bk = full(dve, ("rank", i))
                    dve.tensor_scalar(pa[:, 0, :], bk[:, 0:E], float(CAP), BIG, ALU.is_ge, ALU.mult)
                    dve.tensor_tensor(pa[:, 1, :], bk[:, 0:E], base, ALU.add).then_inc(rank_done, 1)
                    dve.wait_ge(rank_done, i + 1)
                    step(dve.tensor_tensor(pa[:, 0, :], pa[:, 0, :], pa[:, 1, :], ALU.add))
                    step(dve.tensor_tensor(pp[:, :, :], oh[:, :, i, :], pa[:, 0:1, :].to_broadcast([P, TOP, E]), ALU.mult))
                    step(dve.tensor_reduce(pos[:, :, i], pp[:, :, :], AX.X, ALU.add))
                    dve.tensor_copy(posi[:, :, i], pos[:, :, i]).then_inc(pos_done, 1)

            dve.tensor_tensor(dlt[:, :], top[:, :, 1], top[:, :, 0], ALU.subtract).then_inc(dlt_done, 1)
            dve.wait_ge(ex_done, 1)
            step(dve.tensor_scalar(e1[:, :], ex[:, :], 1.0, None, ALU.add))
            step(dve.reciprocal(cw[:, 0, :], e1[:, :]))
            step(dve.tensor_tensor(cw[:, 1, :], ex[:, :], cw[:, 0, :], ALU.mult))
            dve.wait_ge(tot_full, 1)
            step(dve.tensor_tensor(nbm[:, :, :], OB[0][:, 0:E].unsqueeze(2).to_broadcast([P, E, MOST]),
                                   cst[:, C_THR:C_THR + MOST].unsqueeze(1).to_broadcast([P, E, MOST]), ALU.is_gt))
            step(dve.tensor_reduce(nb[:, :], nbm[:, :, :], AX.X, ALU.add))
            step(dve.tensor_tensor_scan(inc[:, :], ones[:, :], nb[:, :], 0.0, ALU.mult, ALU.add))
            step(dve.tensor_tensor(de[:, 0, :], inc[:, :], nb[:, :], ALU.subtract))
            step(dve.tensor_scalar(de[:, 1, :], de[:, 0, :], float(CAP), PRIM - CAP - BIG, ALU.mult, ALU.add))
            step(dve.tensor_tensor(de[:, 2, :], de[:, 1, :], base, ALU.subtract))
            for s in range(TOP):
                ins = dve.tensor_tensor(ohd[:, s, :, :], oh[:, s, :, :], de[:, 2:3, :].to_broadcast([P, T, E]), ALU.mult)
            step(ins)
            dve.tensor_scalar(far[:, :, :], pos[:, :, :], BIG, None, ALU.is_ge)
            step(dve.tensor_reduce(dsel[:, :, :], ohd[:, :, :, :], AX.X, ALU.add))
            step(dve.tensor_tensor(dsel[:, :, :], dsel[:, :, :], far[:, :, :], ALU.mult))
            dve.tensor_scalar(ovf[:, :, :], far[:, :, :], -BIG, BIG, ALU.mult, ALU.add)
            step(dve.tensor_tensor(posg[:, :, :], pos[:, :, :], dsel[:, :, :], ALU.add))
            step(dve.tensor_tensor(ovf[:, :, :], ovf[:, :, :], posg[:, :, :], ALU.add))
            dve.tensor_copy(posgi[:, :, :], posg[:, :, :])
            dve.tensor_copy(ovi[:, :, :], ovf[:, :, :])
            step(dve.tensor_tensor(ejm[:, :, :], inc[:, :].unsqueeze(1).to_broadcast([P, OVB + 1, E]),
                                   cst[:, C_J:C_J + OVB + 1].unsqueeze(2).to_broadcast([P, OVB + 1, E]), ALU.is_le))
            step(dve.tensor_reduce(ejf[:, :], ejm[:, :, :], AX.X, ALU.add))
            step(dve.tensor_copy(ejf[:, OVB:OVB + 1], inc[:, E - 1:E]))
            dve.tensor_scalar(opick[:, :], ejf[0:96, 0:OVB], cst[0:96, C_MOD:C_MOD + 1], None, ALU.is_equal)
            dve.tensor_scalar(ctl[:, :], ejf[:, :], float(E - 1), None, ALU.min).then_inc(ctl_done, 1)

            for u in range(YBUF):
                dve.wait_ge(y_full, u + 1)
                dve.tensor_copy(ye[u], GB[u % 2][:, :]).then_inc(y_done, 1)

            def results(n, u):
                dve.wait_ge(y_full, n * TURN + (u + 1))
                dve.wait_ge(st_y[u % YBUF], n * (16 * (TURN // YBUF)) + 16 * (u // YBUF))
                dve.tensor_copy(ye[u % YBUF], GB[u % 2][:, :]).then_inc(y_done, 1)

            with dve.Fori(0, TURNS - 1) as n:
                for u in range(TURN):
                    results(n, u + YBUF)
            for u in range(YBUF, TURN):
                results(TURNS - 1, u)
            more = dve.value_load(ctl[0:1, OVB:OVB + 1], min_val=0, max_val=OVB)
            with dve.If(more > 0):
                for i in range(YBUF):
                    dve.wait_ge(st_y[i], 16 * TILES // YBUF)
                with dve.Fori(0, OVB) as j:
                    dve.wait_ge(y_full, j + (TILES + 1))
                    dve.wait_ge(st_y[0], j * 16 + 16 * (TILES // YBUF))
                    dve.tensor_copy(ye[0], GB[0][:, :]).then_inc(y_done, 1)
            dve.wait_ge(ld_gb, 16)
            for t in range(T):
                ya, yb = yg[t % 4]
                dve.wait_ge(gath[t % 4], 16 * TOP * (t // 4 + 1))
                dve.wait_ge(ya_done, t + 1)
                step(dve.scalar_tensor_tensor(out=yb, in0=yb, scalar=cw[:, 1, t:t + 1], in1=ya, op0=ALU.mult, op1=ALU.add))
                step(dve.tensor_tensor(yb, yb, bc[:, 0, t // 2, :], ALU.mult))
                dve.tensor_tensor(xt[:, t, :], xt[:, t, :], yb, ALU.add).then_inc(out_done, 1)


def constants():
    import numpy as np
    c = np.zeros((P, C_END), np.float32)
    r = np.arange(P)
    c[:, C_ID:C_ID + P] = np.eye(P)
    c[:, C_MASK:C_MASK + P] = np.where(r[None, :] <= r[:, None], 0.0, -1e20)
    c[:, C_TRI:C_TRI + P] = r[:, None] < r[None, :]
    c[:, C_IOTA:C_IOTA + E] = np.arange(E)
    c[:, C_BASE:C_BASE + E] = np.arange(E) * CAP
    c[:, C_THR:C_THR + MOST] = np.arange(1, MOST + 1) * CAP
    c[:, C_J:C_J + OVB + 1] = np.arange(OVB + 1)
    c[:, C_MOD] = r % E
    inv = (1.0 / np.float32(10000.0) ** (np.arange(0, HD, 2, dtype=np.float32) / np.float32(HD))).astype(np.float32)
    angle = np.arange(S, dtype=np.float32)[:, None] * inv[None, :]
    cos, sin = 0.5 * np.cos(angle), 0.5 * np.sin(angle)
    table = np.stack([np.stack([cos, cos], -1).reshape(S, HD), np.stack([-sin, sin], -1).reshape(S, HD)], 1)
    c[:, C_ROPE:C_END] = table.reshape(QTS, P, 2, HD).transpose(1, 0, 2, 3).reshape(P, -1)
    return c


def kernel(**inputs):
    import numpy as np
    import concourse.bacc as bacc
    from concourse.bass_utils import run_bass_kernel_spmd

    a = {k: np.asarray(v) for k, v in inputs.items()}
    arrays = {
        "x": a["L0_attn_x"].reshape(B * S, D),
        "cT": a["L0_c"].T.reshape(KT, P, B).transpose(1, 0, 2).reshape(P, KT * B),
        "wmod": a["L0_wmod"].reshape(KT, P, NMOD, D).transpose(2, 1, 0, 3).reshape(NMOD, P, KT * D),
        "wqkv": a["L0_attn_w_qkv"].T.reshape(KT, P, QKV).transpose(1, 0, 2),
        "bqkv": a["L0_attn_b_qkv"],
        "wo": a["L0_attn_w_o"].T.reshape(KVH, GROUP, HD, D).transpose(0, 2, 1, 3).reshape(P, GROUP, D),
        "bo": a["L0_attn_b_o"],
        "gate": a["L0_ffn_gate_w"].T.reshape(KT, P, E).transpose(1, 0, 2),
        "ew": a["L0_ffn_expert_w"].transpose(0, 2, 1).reshape(E, KT, P, D).transpose(0, 2, 1, 3).reshape(E, P, KT * D),
        "eb": a["L0_ffn_expert_b"],
        "const": constants(),
    }
    arrays = {f"in_{k}": np.ascontiguousarray(v) for k, v in arrays.items()}
    nc = bacc.Bacc("TRN2", target_bir_lowering=False, num_devices=1)
    args = [nc.dram_tensor(k, v.shape, mybir.dt.from_np(v.dtype), kind="ExternalInput").ap() for k, v in arrays.items()]
    out = nc.dram_tensor("out", (B * S, D), F32, kind="ExternalOutput").ap()
    program(nc, *args, out)
    r = run_bass_kernel_spmd(nc, [arrays], core_ids=[0])
    return r.results[0]["out"].reshape(B, S, D)
```
